# Optimizing a Trainium2 kernel written in Bass

```python
import numpy as np
import jax
import jax.numpy as jnp

def _softmax(x, axis=-1):
    return jax.nn.softmax(x, axis=axis)

def _gelu(x):
    return jax.nn.gelu(x, approximate=True)

def _silu(x):
    return jax.nn.silu(x)

def _sigmoid(x):
    return jax.nn.sigmoid(x)

def _layernorm(x, axis=-1, eps=1e-05):
    m = jnp.mean(x, axis=axis, keepdims=True)
    v = jnp.var(x, axis=axis, keepdims=True)
    return (x - m) / jnp.sqrt(v + eps)

def _scatter_add(tgt, idx, src, axis=0):
    return tgt.at[idx].add(src)

def _segment_sum(src, seg, n):
    return jax.ops.segment_sum(src, seg, n)
kernel_name = 'mk_xattn_ffn_d1_seqx_r4_45cb1f'

def setup_inputs(seed: int=0):
    np.random.seed(seed)
    _w = jnp.asarray

    def _rec_inputs():
        import jax
        import jax.numpy as jnp
        _rk = jax.random.key(seed)
        x = -0.0002928 + 1 * jax.random.normal(jax.random.fold_in(_rk, 1), (32, 256, 256), jnp.float32)
        _lenS = 256 - jax.random.randint(jax.random.fold_in(_rk, 7), (32,), 0, max(1, 256 // 4) + 1, jnp.int32)
        _lenS2 = 77 - jax.random.randint(jax.random.fold_in(_rk, 8), (32,), 0, max(1, 77 // 4) + 1, jnp.int32)
        _ctx_512P = jax.random.normal(jax.random.fold_in(_rk, 11), (32, 16, 128), jnp.float32)
        _ctx_512c = jax.random.dirichlet(jax.random.fold_in(_rk, 511), 0.3 * jnp.ones((16,), jnp.float32), (32, 77))
        _ctx_512t = jnp.einsum('bsk,bkd->bsd', _ctx_512c, _ctx_512P)
        _ctx_512t = _ctx_512t * jax.lax.rsqrt(jnp.mean(jnp.square(_ctx_512t)) + 1e-12) * 0.953939
        ctx_512 = -0.000514642 + 1.00011 * (_ctx_512t + 0.3 * jax.random.normal(jax.random.fold_in(_rk, 611), (32, 77, 128), jnp.float32))
        return (x, ctx_512)
    x, ctx_512 = _rec_inputs()

    def _L0_xattn_setup():
        import jax, jax.numpy as jnp
        import numpy as np
        DIM = 256
        LATENT_DIM = 128
        NUM_HEADS = 16
        HEAD_DIM = DIM // NUM_HEADS
        SCALE = HEAD_DIM ** (-0.5)
        key = jax.random.key(seed)
        k1, k2, k3, k4, k5 = jax.random.split(key, 5)
        B, xN, zN = (2, 512, 512)
        x = jax.random.normal(k1, (B, xN, DIM), dtype=jnp.float32)
        z = jax.random.normal(k2, (B, zN, LATENT_DIM), dtype=jnp.float32)
        Wq = jax.random.normal(k3, (DIM, DIM), dtype=jnp.float32) * DIM ** (-0.5)
        Wkv = jax.random.normal(k4, (2 * DIM, LATENT_DIM), dtype=jnp.float32) * LATENT_DIM ** (-0.5)
        Wo = jax.random.normal(k5, (DIM, DIM), dtype=jnp.float32) * DIM ** (-0.5)
        return {'x': x, 'z': z, 'Wq': Wq, 'Wkv': Wkv, 'Wo': Wo}
    _L0_xattn_all = _L0_xattn_setup()
    _L0_xattn_in = {k: v for k, v in _L0_xattn_all.items() if k in ('Wq', 'Wkv', 'Wo')}
    del _L0_xattn_all

    def _L0_ffn_setup():
        import jax, jax.numpy as jnp
        import numpy as np
        D_MODEL = 256
        EXPERT_DIM = 128
        N_EXPERTS = 8
        TOP_K = 2

        def _sq_relu(h):
            return jnp.square(jax.nn.relu(h))
        key = jax.random.key(seed)
        ks = jax.random.split(key, 6)
        s = 0.02
        x = jax.random.normal(ks[0], (2, 512, D_MODEL), dtype=jnp.float32)
        Ws1 = jax.random.normal(ks[1], (D_MODEL, EXPERT_DIM), dtype=jnp.float32) * s
        Ws2 = jax.random.normal(ks[2], (EXPERT_DIM, D_MODEL), dtype=jnp.float32) * s
        W1 = jax.random.normal(ks[3], (N_EXPERTS, D_MODEL, EXPERT_DIM), dtype=jnp.float32) * s
        W2 = jax.random.normal(ks[4], (N_EXPERTS, EXPERT_DIM, D_MODEL), dtype=jnp.float32) * s
        Wr = jax.random.normal(ks[5], (D_MODEL, N_EXPERTS), dtype=jnp.float32) * s
        return {'x': x, 'Ws1': Ws1, 'Ws2': Ws2, 'W1': W1, 'W2': W2, 'Wr': Wr}
    _L0_ffn_all = _L0_ffn_setup()
    _L0_ffn_in = {k: v for k, v in _L0_ffn_all.items() if k in ('Ws1', 'Ws2', 'W1', 'W2', 'Wr')}
    del _L0_ffn_all
    return {'x': x, 'ctx_512': ctx_512, 'L0_xattn_Wq': _L0_xattn_in['Wq'], 'L0_xattn_Wkv': _L0_xattn_in['Wkv'], 'L0_xattn_Wo': _L0_xattn_in['Wo'], 'L0_ffn_Ws1': _L0_ffn_in['Ws1'], 'L0_ffn_Ws2': _L0_ffn_in['Ws2'], 'L0_ffn_W1': _L0_ffn_in['W1'], 'L0_ffn_W2': _L0_ffn_in['W2'], 'L0_ffn_Wr': _L0_ffn_in['Wr']}

def reference(x, ctx_512, L0_xattn_Wq, L0_xattn_Wkv, L0_xattn_Wo, L0_ffn_Ws1, L0_ffn_Ws2, L0_ffn_W1, L0_ffn_W2, L0_ffn_Wr):
    import jax
    import jax.numpy as jnp

    def _L0_xattn_ref(x, z, Wq, Wkv, Wo):
        import jax, jax.numpy as jnp
        import numpy as np
        DIM = 256
        LATENT_DIM = 128
        NUM_HEADS = 16
        HEAD_DIM = DIM // NUM_HEADS
        SCALE = HEAD_DIM ** (-0.5)
        B, xN, _ = x.shape
        _, zN, _ = z.shape
        Q = (x @ Wq.T).reshape(B, xN, NUM_HEADS, HEAD_DIM)
        KV = (z @ Wkv.T).reshape(B, zN, 2, NUM_HEADS, HEAD_DIM)
        K = KV[:, :, 0]
        V = KV[:, :, 1]
        attn = jnp.einsum('bqhd,bkhd->bhqk', Q, K) * SCALE
        attn = jax.nn.softmax(attn, axis=-1)
        O = jnp.einsum('bhqk,bkhd->bqhd', attn, V).reshape(B, xN, DIM)
        return O @ Wo.T

    def _L0_ffn_ref(x, Ws1, Ws2, W1, W2, Wr):
        import jax, jax.numpy as jnp
        import numpy as np
        D_MODEL = 256
        EXPERT_DIM = 128
        N_EXPERTS = 8
        TOP_K = 2

        def _sq_relu(h):
            return jnp.square(jax.nn.relu(h))
        shape = x.shape
        xf = x.reshape(-1, D_MODEL)
        out_shared = _sq_relu(xf @ Ws1) @ Ws2
        logits = xf @ Wr
        top_vals, top_idx = jax.lax.top_k(logits, TOP_K)
        rw = jax.nn.softmax(top_vals.astype(jnp.float32), axis=-1).astype(x.dtype)
        onehot = jax.nn.one_hot(top_idx, N_EXPERTS, dtype=x.dtype)
        prob = jnp.einsum('tk,tke->te', rw, onehot)
        prob = jnp.trunc(prob)
        h = _sq_relu(jnp.einsum('td,edf->tef', xf, W1))
        y = jnp.einsum('tef,efd->ted', h, W2)
        out_routed = jnp.einsum('ted,te->td', y, prob)
        return (out_shared + out_routed).reshape(shape)
    x = x + _L0_xattn_ref(_layernorm(x, axis=-1), ctx_512, L0_xattn_Wq, L0_xattn_Wkv, L0_xattn_Wo)
    x = x + _L0_ffn_ref(_layernorm(x, axis=-1), L0_ffn_Ws1, L0_ffn_Ws2, L0_ffn_W1, L0_ffn_W2, L0_ffn_Wr)
    return x

_drawn_inputs = setup_inputs


def setup_inputs(seed=0):
    import zlib

    import numpy as np

    out = dict(_drawn_inputs(seed))
    spreads = {}
    factors = {}
    for name, (base, spread) in spreads.items():
        noise = np.random.default_rng([zlib.crc32(name.encode()), seed]).standard_normal(out[name].shape)
        drawn = base * np.exp(spread * noise) if base else spread * noise
        out[name] = jnp.asarray(drawn.astype(out[name].dtype))
    for name, factor in factors.items():
        out[name] = (out[name] * factor).astype(out[name].dtype)
    return out
```

```python
import concourse.bass as bass
from concourse import mybir
from concourse.alu_op_type import AluOpType as ALU
from contextlib import ExitStack

FP32 = mybir.dt.float32
FP32R = mybir.dt.float32r
BF16 = mybir.dt.bfloat16
FP16 = mybir.dt.float16
I32 = mybir.dt.int32
ACT = mybir.ActivationFunctionType
AX = mybir.AxisListType

P = 128
NB, S, D = 32, 256, 256
NT = NB * S // P
LAT, NK = 128, 77
H, HD = 16, 16
F, NE = 128, 8
EPS = 1e-5
SCALE = HD ** -0.5
BIG = 3.0e38

PARTS = 3
HR = PARTS * HD
MROW = 2 * HR
CUT = P - NK
REST = NK - CUT
ZW = 2 * NK + REST
NSL = 11
FIRST = [3 * (s // 2) + s % 2 for s in range(NSL)]
NHS = [min(2, H - f) for f in FIRST]
VBLK = [2 * (s // 2) if s % 2 == 0 else 11 + 2 * (s // 2) for s in range(NSL)]
NBLK = 21
GROUPS = [(2 * j, min(2, NSL - 2 * j)) for j in range(6)]
NCONST = 9
OC = HD + 1
HG = 4 * NK
KB = 4
NKC = NB // KB
KC = KB * NK
DMA = 16


class Batch:

    def __init__(self, i, k):
        self.i, self.k = i, k

    def __add__(self, d):
        return Batch(self.i, self.k + d)

    @property
    def par(self):
        return self.k % 2

    def at(self, per, j):
        return self.i * (2 * per) + (self.k * per + j)

    def at2(self, per):
        return self.i * per + (self.k // 2 + 1) * per

    def index(self):
        return self.i * 2 + self.k


LOOP_FROM, LOOP_TO = 2, 30


def schedule(eng, step):
    def static(s):
        step(Batch(0, s), 0 <= s + 2 < NB, 0 <= s + 1 < NB, 0 <= s < NB, 0 <= s - 1 < NB)
    for s in range(-2, LOOP_FROM):
        static(s)
    with eng.Fori(LOOP_FROM // 2, LOOP_TO // 2) as i:
        step(Batch(i, 0), True, True, True, True)
        step(Batch(i, 1), True, True, True, True)
    for s in range(LOOP_TO, NB + 1):
        static(s)


def build(nc, x_d, z_d, zz_d, wq_d, wk_d, wv_d, wo_d, w1r_d, ws2_d, w1_d, w2_d, ident_d, mask_d, headmask_d, sel_d, out_d):
    kt_d = nc.dram_tensor("kt_scratch", (2 * P, PARTS, NB * NK), FP32, kind="Internal").ap()
    qt_d = nc.dram_tensor("qt_scratch", (2, (H + 2) * HD, PARTS, S), FP32, kind="Internal").ap()
    ctx = ExitStack()
    with ctx:
        def sb(name, shape, dt=FP32):
            return ctx.enter_context(nc.sbuf_tensor(name, shape, dt))

        def sem(name):
            return ctx.enter_context(nc.semaphore(name))

        def sem2(name):
            return [sem(f"{name}{p}") for p in range(2)]

        X = sb("X", [P, NT, D])
        zw = sb("zw", [P, 2 * NE * F + NE * D])
        z = zw[:, 0:NB * NK].rearrange("p (b k) -> p b k", k=NK)
        sel = zw[:, NB * NK:NB * NK + NSL * P]
        w1 = zw[:, 0:2 * NE * F].rearrange("p (k e f) -> p k e f", k=2, e=NE)
        w2 = zw[:, 2 * NE * F:].rearrange("p (e d) -> p e d", e=NE)
        zc = sb("zc", [P, 2, ZW])
        wq = sb("wq", [P, 2, D])
        wk = sb("wk", [P, D])
        wv = sb("wv", [P, NBLK * HD])
        wo = sb("wo", [P, 2, D])
        w1r = sb("w1r", [P, 2, F + NE])
        ws2 = sb("ws2", [P, D])
        ident = sb("ident", [P, P])
        mask = sb("mask", [P, NBLK])
        kth = sb("kth", [P, 2, 2, KC], FP32R)
        ktl = sb("ktl", [P, 2, 2, KC], FP32R)
        kT = sb("kT", [P, 2, 2, NK])
        headmask = sb("headmask", [P, 8])
        kbd = sb("kbd", [P, 2, 2, 8 * NK], FP32R)
        kst = sb("kst", [P, 2, NSL, P], FP32R)
        qst = sb("qst", [P, 2, NSL, S], FP32R)
        st1 = sb("st1", [P, 2, 6])
        mv1 = sb("mv1", [P, 2, 2])
        ve1 = sb("ve1", [P, 2])
        rs1 = sb("rs1", [P, 2])
        nb1 = sb("nb1", [P, 2])
        st2 = sb("st2", [P, 2, 6])
        mv2 = sb("mv2", [P, 2, 2])
        ve2 = sb("ve2", [P, 2])
        rs2 = sb("rs2", [P, 2])
        nb2 = sb("nb2", [P, 2])
        mhalf = sb("mhalf", [P, 2])
        xn = sb("xn", [P, 2, 2, D])
        xnT = sb("xnT", [P, 2, S])
        qh = sb("qh", [P, 2, 2, S], FP32R)
        ql = sb("ql", [P, 2, 2, S], FP32R)
        nm = sb("nm", [P, 2, H])
        mh = sb("mh", [H, S], FP32R)
        vf = sb("vf", [P, NBLK, HD])
        vr = sb("vr", [P, NBLK, HD])
        v1 = sb("v1", [P, 2, NBLK, OC], BF16)
        v2 = sb("v2", [P, 2, NBLK, OC], BF16)
        v3 = sb("v3", [P, 2, NBLK, OC], BF16)
        E = sb("E", [P, 2, 2, S])
        ph = sb("ph", [P, 2, 2, S], FP16)
        pl = sb("pl", [P, 2, 2, S], FP16)
        rden = sb("rden", [P, 2, H])
        on = sb("on", [P, 2, D])
        onT = sb("onT", [P, 2, S])
        yn = sb("yn", [P, 2, D])
        ynT = sb("ynT", [P, 2, S])
        hr = sb("hr", [P, 2, F])
        hT = sb("hT", [P, S])
        ost = sb("ost", [P, 2, 2, D])
        logits = sb("logits", [P, NT, NE])
        prob = sb("prob", [P, NT, NE])
        top = sb("top", [P, 5, NT])
        ones = sb("ones", [P, 1])
        any1 = sb("any1", [P, 1])
        flag = sb("flag", [1, 1], I32)
        l2 = sb("l2", [P, NT, NE])
        gout = sb("gout", [P, D])

        def pb(name, cols):
            return ctx.enter_context(nc.psum_tensor(name, [P, cols], FP32))

        psS = [pb(f"psS{j}", 512) for j in range(2)]
        psO = [pb(f"psO{j}", 512) for j in range(2)]
        psA = pb("psA", 1024)
        M0, M1 = pb("M0", 512), pb("M1", 512)

        consts_in = sem("consts_in")
        const1_in = sem("const1_in")
        experts_in = sem("experts_in")
        x_in = sem2("x_in")
        zc_in = sem2("zc_in")
        kT_in = sem2("kT_in")
        qt_stored = sem2("qt_stored")
        pad_stored = sem("pad_stored")
        kbd_ready = sem("kbd_ready")
        kst_in = sem2("kst_in")
        qst_in = sem2("qst_in")
        m_in = sem2("m_in")
        out_stored = sem2("out_stored")
        kt_stored = sem2("kt_stored")
        zeroed = sem("zeroed")
        kst_ready = sem("kst_ready")
        kproj, kth_ready, ktl_ready = sem("kproj"), sem("kth_ready"), sem("ktl_ready")
        stats1, scale1, xn_ready = sem("stats1"), sem("scale1"), sem("xn_ready")
        v_done, v_masked, v_ready = sem("v_done"), sem("v_masked"), sem("v_ready")
        pool_step = sem("pool_step")
        ln1_step, ln2_step = sem("ln1_step"), sem("ln2_step")
        xT_done, xnT_ready = sem("xT_done"), sem("xnT_ready")
        q_done, qh_ready, ql_ready = sem("q_done"), sem("qh_ready"), sem("ql_ready")
        sa_done, max_ready = sem("sa_done"), sem("max_ready")
        mT_done, mh_ready = sem("mT_done"), sem("mh_ready")
        s_done, e_ready, ph_ready, pl_ready = sem("s_done"), sem("e_ready"), sem("ph_ready"), sem("pl_ready")
        pv_done, den_ready, on_ready = sem("pv_done"), sem("den_ready"), sem("on_ready")
        oT_done, onT_ready = sem("oT_done"), sem("onT_ready")
        attn_done, y_ready = sem("attn_done"), sem("y_ready")
        stats2, scale2, yn_ready = sem("stats2"), sem("scale2"), sem("yn_ready")
        yT_done, ynT_ready = sem("yT_done"), sem("ynT_ready")
        h_done, hr_ready, logits_ready = sem("h_done"), sem("hr_ready"), sem("logits_ready")
        hT_done, hT_ready = sem("hT_done"), sem("hT_ready")
        ffn_done, out_ready = sem("ffn_done"), sem("out_ready")
        top_step, gap_exp, any_done, flag_ready = sem("top_step"), sem("gap_exp"), sem("any_done"), sem("flag_ready")
        E_ = mybir.EngineType
        passed = {e: sem(f"passed_{e.name}") for e in (E_.SP, E_.DVE, E_.Pool)}
        g_out_in, g_stored, g_added = sem("g_out_in"), sem("g_stored"), sem("g_added")
        g_step, g_stats, g_scale, g_yn = sem("g_step"), sem("g_stats"), sem("g_scale"), sem("g_yn")
        g_yT, g_ynT, g_h, g_relu = sem("g_yT"), sem("g_ynT"), sem("g_h"), sem("g_relu")
        g_hT, g_y = sem("g_hT"), sem("g_y")

        def stand_alone(eng):
            eng.sem_inc(passed[eng.engine], 1)

        x_t = x_d.rearrange("(n j p) d -> p n j d", p=P, j=2)
        out_t = out_d.rearrange("(n j p) d -> p n j d", p=P, j=2)

        block = ctx.enter_context(nc.Block())

        @block.sync
        def _(sp):
            sp.dma_start(z[:, :, :], z_d).then_inc(consts_in, DMA)
            sp.dma_start(wk[:, :], wk_d).then_inc(consts_in, DMA)
            for b in range(2):
                sp.dma_start(X[:, 2 * b:2 * b + 2, :], x_t[:, b]).then_inc(x_in[b], DMA)
                sp.dma_start(zc[:, b, :], zz_d[:, b, :]).then_inc(zc_in[b], DMA)
            for dst, src in ((sel[MROW:P, :], sel_d), (mask[:, :], mask_d), (headmask[:, :], headmask_d), (ident[:, :], ident_d),
                             (wq[:, :, :], wq_d), (wv[:, :], wv_d), (wo[:, :, :], wo_d),
                             (w1r[:, :, :], w1r_d), (ws2[:, :], ws2_d)):
                sp.dma_start(dst, src).then_inc(const1_in, DMA)
            for c in range(NKC):
                p = c % 2
                cols = slice(c * KC, (c + 1) * KC)
                if c >= 2:
                    sp.wait_ge(kt_stored[p], PARTS * DMA * (c // 2))
                dst = kt_d[:, :, cols].rearrange("(h p) n c -> p h n c", p=P)
                sp.wait_ge(kth_ready, 2 * (c + 1))
                for n in range(2):
                    sp.dma_start(dst[:, :, n, :], kth[:, p, :, :].bitcast(FP32)).then_inc(kt_stored[p], DMA)
                sp.wait_ge(ktl_ready, 2 * (c + 1))
                sp.dma_start(dst[:, :, 2, :], ktl[:, p, :, :].bitcast(FP32)).then_inc(kt_stored[p], DMA)
            sp.wait_ge(zeroed, 4)
            for p in range(2):
                sp.dma_start(qt_d[p, H * HD:(H + 1) * HD].rearrange("r n q -> (r n) q"),
                             qst[0:HR, p, 0, :].bitcast(FP32)).then_inc(pad_stored, DMA)
            for p in range(2):
                sp.wait_ge(kt_stored[p], PARTS * DMA * (NKC // 2))
            sp.wait_ge(pad_stored, 2 * DMA)
            sp.wait_ge(kst_ready, 2)

            kt_rows = kt_d.rearrange("r n (b k) -> (r n) b k", k=NK).rearrange("(i r) b k -> r i b k", r=HR)
            kt_high = kt_d[:, 0, :].rearrange("(h p) (b k) -> p h b k", p=P, k=NK)

            def load_kT(b):
                sp.dma_start(kT[:, b.par, :, :], kt_high[:, :, bass.ds(b.index(), 1), :].rearrange("p h b k -> p h (b k)")
                             ).then_inc(kT_in[b.par], DMA)

            def load_kst(b):
                roles = ((0, 0, 6, 0, 0, NK, 0), (1, 0, 5, HR, NK, P, 0),
                         (1, 1, 5, 0, 0, REST, CUT), (2, 1, 5, HR, REST, REST + NK, 0))
                for head, first, n, r, c0, c1, k0 in roles:
                    src = kt_rows[:, head:head + 3 * (n - 1) + 1:3, bass.ds(b.index(), 1), k0:k0 + c1 - c0]
                    sp.dma_start(kst[r:r + HR, b.par, first:first + 2 * (n - 1) + 1:2, c0:c1].bitcast(FP32),
                                 src.rearrange("r i b k -> r i (b k)")).then_inc(kst_in[b.par], DMA)

            def store_q(b, part, n):
                sp.dma_start(qt_d[b.par, 0:H * HD, n, :].rearrange("(h p) q -> p h q", p=P),
                             part[:, b.par, :, :].bitcast(FP32)).then_inc(qt_stored[b.par], DMA)

            def stack_q(b):
                src = qt_d[b.par].rearrange("r n q -> (r n) q").rearrange("(i r) q -> r i q", r=3 * HR)
                sp.dma_start(qst[0:2 * HR, b.par, 0:NSL:2, :].bitcast(FP32), src[0:2 * HR]).then_inc(qst_in[b.par], DMA)
                sp.dma_start(qst[0:2 * HR, b.par, 1:NSL:2, :].bitcast(FP32), src[HR:3 * HR, 0:5]).then_inc(qst_in[b.par], DMA)

            load_kT(Batch(0, 0))
            load_kT(Batch(0, 1))

            def step(b, L, A, C, D_):
                if L and not (isinstance(b.i, int) and b.k < 0):
                    nx = b + 2
                    sp.wait_ge(x_in[nx.par], b.at2(DMA))
                    stand_alone(sp)
                    sp.dma_start(X[:, bass.ds(nx.index() * 2, 2), :],
                                 x_t[:, bass.ds(nx.index(), 1)].rearrange("p n j d -> p (n j) d")
                                 ).then_inc(x_in[nx.par], DMA)
                    sp.wait_ge(v_done, b.at(1, 1))
                    stand_alone(sp)
                    sp.dma_start(zc[:, nx.par, :], zz_d[:, bass.ds(nx.index(), 1), :].rearrange("p b c -> p (b c)")
                                 ).then_inc(zc_in[nx.par], DMA)
                    sp.wait_ge(kbd_ready, b.at(2, 2))
                    stand_alone(sp)
                    load_kT(nx)
                if A:
                    na = b + 1
                    if not (isinstance(b.i, int) and b.k < 1):
                        sp.wait_ge(s_done, (b + -1).at(6, 6))
                        stand_alone(sp)
                        sp.wait_ge(kst_in[na.par], (b + -1).at2(4 * DMA))
                        stand_alone(sp)
                        sp.wait_ge(qst_in[na.par], (b + -1).at2(2 * DMA))
                        stand_alone(sp)
                        sp.wait_ge(m_in[na.par], (b + -1).at2(DMA))
                    stand_alone(sp)
                    load_kst(na)
                    sp.wait_ge(qh_ready, na.at(1, 1))
                    stand_alone(sp)
                    store_q(na, qh, 0)
                    store_q(na, qh, 2)
                    sp.wait_ge(ql_ready, na.at(1, 1))
                    stand_alone(sp)
                    store_q(na, ql, 1)
                    sp.wait_ge(qt_stored[na.par], na.at2(PARTS * DMA))
                    stand_alone(sp)
                    stack_q(na)
                    sp.wait_ge(mh_ready, na.at(1, 1))
                    stand_alone(sp)
                    sp.dma_start(qst[MROW:MROW + H, na.par, :, :].bitcast(FP32),
                                 mh[:, :].bitcast(FP32).unsqueeze(1).to_broadcast([H, NSL, S])).then_inc(m_in[na.par], DMA)
                if D_:
                    d = b + -1
                    sp.wait_ge(out_ready, d.at(1, 1))
                    stand_alone(sp)
                    sp.dma_start(out_t[:, bass.ds(d.index(), 1)].rearrange("p n j d -> p (n j) d"),
                                 ost[:, d.par, :, :]).then_inc(out_stored[d.par], DMA)

            schedule(sp, step)
            for p in range(2):
                sp.wait_ge(out_stored[p], DMA * NB // 2)
            sp.wait_ge(flag_ready, 1)
            with sp.If(sp.value_load(flag[0:1, 0:1]) != 0):
                sp.dma_start(w1[:, :, :, :], w1_d).then_inc(experts_in, DMA)
                sp.dma_start(w2[:, :, :], w2_d).then_inc(experts_in, DMA)
                out_n = out_d.rearrange("(n p) d -> p n d", p=P)
                sp.sem_inc(g_stored, DMA)
                with sp.Fori(0, NT) as t:
                    sp.wait_ge(g_stored, t * DMA + DMA)
                    stand_alone(sp)
                    sp.dma_start(gout[:, :], out_n[:, bass.ds(t, 1), :].rearrange("p n d -> p (n d)")).then_inc(g_out_in, DMA)
                    sp.wait_ge(g_added, t * NE + (NE + 1))
                    stand_alone(sp)
                    sp.dma_start(out_n[:, bass.ds(t, 1), :].rearrange("p n d -> p (n d)"), gout[:, :]).then_inc(g_stored, DMA)
                sp.wait_ge(g_stored, NT * DMA + DMA)

        @block.gpsimd
        def _(pool):
            for t in (qst, kst):
                nc.gpsimd.memset(t[:, 0].bitcast(FP32), 0.0).then_inc(zeroed, 1)
                nc.gpsimd.memset(t[:, 1].bitcast(FP32), 0.0).then_inc(zeroed, 1)
            nc.gpsimd.memset(mhalf[:, :], -0.5).then_inc(pool_step, 1)
            nc.gpsimd.memset(ones[:, :], 1.0).then_inc(pool_step, 1)
            nc.gpsimd.memset(v2[:, :, :, :], 0.0).then_inc(pool_step, 1)
            nc.gpsimd.memset(v3[:, :, :, :], 0.0).then_inc(pool_step, 1)
            pool.wait_ge(const1_in, NCONST * DMA)
            for p in range(2):
                nc.gpsimd.tensor_copy(v1[:, p, :, HD:OC], mask[:, :].unsqueeze(2)).then_inc(pool_step, 1)
            pool.wait_ge(pool_step, 6)

            def rsqrt(stats, scale, mv, ve, rs, nb, bt):
                pool.wait_ge(stats, bt.at(2, 2))
                if not (isinstance(bt.i, int) and bt.k < 1):
                    pool.wait_ge(xn_ready if scale is scale1 else yn_ready, (bt + -1).at(1, 1))
                stand_alone(pool)
                nc.gpsimd.tensor_scalar(ve[:, :], mv[:, :, 1], EPS, 1.0, ALU.add, ALU.mult).then_inc(scale, 1)
                pool.wait_ge(scale, bt.at(4, 1))
                nc.gpsimd.tensor_tensor(rs[:, :], ve[:, :], mhalf[:, :], ALU.pow).then_inc(scale, 1)
                pool.wait_ge(scale, bt.at(4, 2))
                stand_alone(pool)
                for j in range(2):
                    nc.gpsimd.tensor_scalar(nb[:, j:j + 1], rs[:, j:j + 1], mv[:, j, 0:1], -1.0,
                                            ALU.mult, ALU.mult).then_inc(scale, 1)

            def split_v(b):
                pool.wait_ge(v_masked, b.at(1, 1))
                if not (isinstance(b.i, int) and b.k < 2):
                    pool.wait_ge(pv_done, (b + -2).at(6, 6))
                stand_alone(pool)
                p = b.par
                nc.gpsimd.tensor_copy(v1[:, p, :, 0:HD], vf[:, :, :]).then_inc(v_ready, 1)
                pool.wait_ge(v_ready, b.at(4, 1))
                nc.gpsimd.tensor_tensor(vr[:, :, :], vf[:, :, :], v1[:, p, :, 0:HD], ALU.subtract).then_inc(v_ready, 1)
                pool.wait_ge(v_ready, b.at(4, 2))
                stand_alone(pool)
                nc.gpsimd.tensor_copy(v2[:, p, :, 0:HD], vr[:, :, :]).then_inc(v_ready, 1)
                pool.wait_ge(v_ready, b.at(4, 3))
                nc.gpsimd.tensor_tensor(v3[:, p, :, 0:HD], vr[:, :, :], v2[:, p, :, 0:HD], ALU.subtract).then_inc(v_ready, 1)

            def diagonal_keys(b):
                pool.wait_ge(kT_in[b.par], b.at2(DMA))
                stand_alone(pool)
                if not (isinstance(b.i, int) and b.k < 2):
                    pool.wait_ge(sa_done, (b + -2).at(4, 4))
                    stand_alone(pool)
                for h in range(2):
                    nc.gpsimd.tensor_tensor(kbd[:, b.par, h, :].rearrange("p (h k) -> p h k", k=NK),
                                            kT[:, b.par, h, :].unsqueeze(1).to_broadcast([P, 8, NK]),
                                            headmask[:, :].unsqueeze(2).to_broadcast([P, 8, NK]), ALU.mult).then_inc(kbd_ready, 1)

            def step(b, L, A, C, D_):
                if A:
                    split_v(b + 1)
                if D_:
                    rsqrt(stats2, scale2, mv2, ve2, rs2, nb2, b + -1)
                if L:
                    rsqrt(stats1, scale1, mv1, ve1, rs1, nb1, b + 2)
                    diagonal_keys(b + 2)

            schedule(pool, step)
            pool.wait_ge(flag_ready, 1)
            with pool.If(pool.value_load(flag[0:1, 0:1]) != 0):
                with pool.Fori(0, NT) as t:
                    pool.wait_ge(g_stats, t + 1)
                    stand_alone(pool)
                    nc.gpsimd.tensor_scalar(ve2[:, 0:1], mv2[:, 0, 1:2], EPS, 1.0, ALU.add, ALU.mult).then_inc(g_scale, 1)
                    pool.wait_ge(g_scale, t * 3 + 1)
                    nc.gpsimd.tensor_tensor(rs2[:, 0:1], ve2[:, 0:1], mhalf[:, 0:1], ALU.pow).then_inc(g_scale, 1)
                    pool.wait_ge(g_scale, t * 3 + 2)
                    stand_alone(pool)
                    nc.gpsimd.tensor_scalar(nb2[:, 0:1], rs2[:, 0:1], mv2[:, 0, 0:1], -1.0, ALU.mult, ALU.mult).then_inc(g_scale, 1)

        @block.scalar
        def _(act):
            for c in range(NKC):
                for h in range(2):
                    n = 2 * c + h
                    act.wait_ge(kproj, n + 1)
                    if c >= 2:
                        act.wait_ge(kt_stored[c % 2], PARTS * DMA * (c // 2))
                    nc.scalar.activation(kth[:, c % 2, h, :], psA[:, 512 * h:512 * h + KC], ACT.Copy).then_inc(kth_ready, 1)
            act.wait_ge(const1_in, NCONST * DMA)
            act.wait_ge(zeroed, 4)
            for p in range(2):
                nc.scalar.activation(kst[MROW:P, p, :, :].rearrange("r s c -> r (s c)"), sel[MROW:P, :],
                                     ACT.Copy).then_inc(kst_ready, 1)

            def step(b, L, A, C, D_):
                na, d, nl = b + 1, b + -1, b + 2

                def exps(j):
                    s0, n = GROUPS[j]
                    act.wait_ge(s_done, b.at(6, j + 1))
                    e = (6 * b.par + j) % 2
                    if not (isinstance(b.i, int) and b.k < 1 and j < 2):
                        act.wait_ge(pl_ready, b.at(6, j - 1))
                    nc.scalar.activation(E[:, e, 0:n, :], psS[e][:, 0:n * S].rearrange("p (n q) -> p n q", n=n),
                                         ACT.Exp, scale=SCALE).then_inc(e_ready, 1)
                    if not (isinstance(b.i, int) and b.k < 1 and j < 2):
                        act.wait_ge(pv_done, b.at(6, j - 1))
                    nc.scalar.activation(ph[:, e, 0:n, :], psS[e][:, 0:n * S].rearrange("p (n q) -> p n q", n=n),
                                         ACT.Exp, scale=SCALE).then_inc(ph_ready, 1)

                if A:
                    act.wait_ge(xT_done, na.at(1, 1))
                    nc.scalar.activation(xnT[:, :, :], M1[:, :].rearrange("p (k q) -> p k q", k=2), ACT.Copy).then_inc(xnT_ready, 1)
                if C:
                    exps(0)
                if D_:
                    act.wait_ge(oT_done, d.at(1, 1))
                    nc.scalar.activation(onT[:, :, :], M0[:, :].rearrange("p (k q) -> p k q", k=2), ACT.Copy).then_inc(onT_ready, 1)
                if A:
                    act.wait_ge(q_done, na.at(1, 1))
                    if not (isinstance(na.i, int) and na.k < 2):
                        act.wait_ge(qst_in[na.par], (na + -2).at2(2 * DMA))
                    nc.scalar.activation(qh[:, na.par, :, :], M1[:, :].rearrange("p (k q) -> p k q", k=2), ACT.Copy).then_inc(qh_ready, 1)
                if C:
                    exps(1)
                    exps(2)
                    exps(3)
                if D_:
                    act.wait_ge(scale2, d.at(4, 4))
                    for j in range(2):
                        last = nc.scalar.activation(yn[:, j, :], X[:, bass.ds(d.index() * 2 + j, 1), :].rearrange("p a c -> p (a c)"),
                                                    ACT.Identity, scale=rs2[:, j:j + 1], bias=nb2[:, j:j + 1])
                    last.then_inc(yn_ready, 1)
                    act.wait_ge(yT_done, d.at(1, 1))
                    nc.scalar.activation(ynT[:, :, :], M1[:, :].rearrange("p (k q) -> p k q", k=2), ACT.Copy).then_inc(ynT_ready, 1)
                if A:
                    act.wait_ge(mT_done, na.at(1, 1))
                    if not (isinstance(na.i, int) and na.k < 1):
                        act.wait_ge(m_in[b.par], b.at2(DMA))
                    nc.scalar.activation(mh[:, :], M0[0:H, 0:S], ACT.Copy).then_inc(mh_ready, 1)
                if C:
                    exps(4)
                if D_:
                    act.wait_ge(h_done, d.at(1, 1))
                    nc.scalar.activation(hr[:, :, :], M1[:, 0:2 * (F + NE)].rearrange("p (j f) -> p j f", j=2)[:, :, 0:F],
                                         ACT.Relu).then_inc(hr_ready, 1)
                if C:
                    exps(5)
                if D_:
                    act.wait_ge(hT_done, d.at(1, 1))
                    nc.scalar.activation(hT[:, :], M0[:, 0:S], ACT.Square).then_inc(hT_ready, 1)
                if L:
                    act.wait_ge(scale1, nl.at(4, 4))
                    if not (isinstance(nl.i, int) and nl.k < 2):
                        act.wait_ge(xT_done, b.at(1, 1))
                    for j in range(2):
                        last = nc.scalar.activation(xn[:, nl.par, j, :], X[:, bass.ds(nl.index() * 2 + j, 1), :].rearrange("p a c -> p (a c)"),
                                                    ACT.Identity, scale=rs1[:, j:j + 1], bias=nb1[:, j:j + 1])
                    last.then_inc(xn_ready, 1)

            schedule(act, step)
            act.wait_ge(top_step, 6)
            nc.scalar.activation(top[:, 3, :], top[:, 2, :], ACT.Exp).then_inc(gap_exp, 1)
            act.wait_ge(flag_ready, 1)
            with act.If(act.value_load(flag[0:1, 0:1]) != 0):
                act.sem_inc(g_hT, 1)
                with act.Fori(0, NT) as t:
                    act.wait_ge(g_scale, t * 3 + 3)
                    nc.scalar.activation(yn[:, 0, :], X[:, bass.ds(t, 1), :].rearrange("p a c -> p (a c)"),
                                         ACT.Identity, scale=rs2[:, 0:1], bias=nb2[:, 0:1]).then_inc(g_yn, 1)
                    act.wait_ge(g_yT, t + 1)
                    nc.scalar.activation(ynT[:, :, 0:P], M0[:, 0:2 * P].rearrange("p (k q) -> p k q", k=2), ACT.Copy).then_inc(g_ynT, 1)
                    for e in range(NE):
                        act.wait_ge(g_h, t * NE + (e + 1))
                        nc.scalar.activation(hr[:, 0, :], M1[:, 0:P], ACT.Relu).then_inc(g_relu, 1)
                        act.wait_ge(g_relu, t * NE + (e + 1))
                        nc.scalar.activation(hT[:, 0:P], hr[:, 0, :], ACT.Square).then_inc(g_hT, 1)

        @block.vector
        def _(dve):
            for c in range(NKC):
                for h in range(2):
                    n = 2 * c + h
                    dve.wait_ge(kth_ready, n + 1)
                    if c >= 2:
                        dve.wait_ge(kt_stored[c % 2], PARTS * DMA * (c // 2))
                    nc.vector.tensor_tensor(ktl[:, c % 2, h, :], psA[:, 512 * h:512 * h + KC],
                                            kth[:, c % 2, h, :].bitcast(FP32), ALU.subtract).then_inc(ktl_ready, 1)

            def step(b, L, A, C, D_):
                na, d, nl = b + 1, b + -1, b + 2

                def low_part(j):
                    s0, n = GROUPS[j]
                    e = (6 * b.par + j) % 2
                    dve.wait_ge(ph_ready, b.at(6, j + 1))
                    if not (isinstance(b.i, int) and b.k < 1 and j < 2):
                        dve.wait_ge(pv_done, b.at(6, j - 1))
                    nc.vector.tensor_tensor(pl[:, e, 0:n, :], E[:, e, 0:n, :], ph[:, e, 0:n, :], ALU.subtract).then_inc(pl_ready, 1)

                def maximum(j):
                    t, h = j // 2, j % 2
                    dve.wait_ge(sa_done, na.at(4, j + 1))
                    if j == 0 and not (isinstance(na.i, int) and na.k < 1):
                        dve.wait_ge(mT_done, b.at(1, 1))
                    src = psA[:, :].rearrange("p (g c) -> p g c", g=2)[:, :, 0:HG].rearrange("p g (h k) -> p g h k", k=NK)
                    nc.vector.tensor_reduce(nm[:, t, 8 * h:8 * h + 8].rearrange("p (g h) -> p g h", g=2), src, AX.X, ALU.max, negate=True).then_inc(max_ready, 1)

                if D_:
                    for t in range(2):
                        o = psO[t][:, 0:H * OC].rearrange("p (h c) -> p h c", c=OC)
                        dve.wait_ge(pv_done, d.at(6, 6))
                        nc.vector.reciprocal(rden[:, t, :].unsqueeze(2), o[:, :, HD:OC]).then_inc(den_ready, 1)
                    for t in range(2):
                        o = psO[t][:, 0:H * OC].rearrange("p (h c) -> p h c", c=OC)
                        dve.wait_ge(den_ready, d.at(2, t + 1))
                        if t == 0 and not (isinstance(d.i, int) and d.k < 1):
                            dve.wait_ge(oT_done, (d + -1).at(1, 1))
                        nc.vector.tensor_tensor(on[:, t, :].rearrange("p (h c) -> p h c", c=HD), o[:, :, 0:HD],
                                                rden[:, t, :].unsqueeze(2).to_broadcast([P, H, HD]), ALU.mult).then_inc(on_ready, 1)
                if A:
                    dve.wait_ge(v_done, na.at(1, 1))
                    if not (isinstance(na.i, int) and na.k < 1):
                        dve.wait_ge(v_ready, b.at(4, 4))
                    nc.vector.tensor_tensor(vf[:, :, :], M0[:, 0:NBLK * HD].rearrange("p (n c) -> p n c", c=HD),
                                            mask[:, :].unsqueeze(2).to_broadcast([P, NBLK, HD]), ALU.mult).then_inc(v_masked, 1)
                if C:
                    low_part(0)
                if A:
                    dve.wait_ge(qh_ready, na.at(1, 1))
                    if not (isinstance(na.i, int) and na.k < 2):
                        dve.wait_ge(qst_in[na.par], (na + -2).at2(2 * DMA))
                    nc.vector.tensor_tensor(ql[:, na.par, :, :], M1[:, :].rearrange("p (k q) -> p k q", k=2),
                                            qh[:, na.par, :, :].bitcast(FP32), ALU.subtract).then_inc(ql_ready, 1)
                if C:
                    low_part(1)
                if A:
                    maximum(0)
                if D_:
                    dve.wait_ge(attn_done, d.at(1, 1))
                    xt = X[:, bass.ds(d.index() * 2, 2), :]
                    nc.vector.tensor_tensor(xt, M0[:, :].rearrange("p (j c) -> p j c", j=2), xt, ALU.add).then_inc(y_ready, 1)
                    dve.wait_ge(y_ready, d.at(1, 1))
                    if not (isinstance(d.i, int) and d.k < 1):
                        dve.wait_ge(scale2, (d + -1).at(4, 4))
                    stand_alone(dve)
                    for j in range(2):
                        nc.vector.bn_stats(st2[:, j, :], X[:, bass.ds(d.index() * 2 + j, 1), :].rearrange("p a c -> p (a c)")).then_inc(ln2_step, 1)
                    dve.wait_ge(ln2_step, d.at(2, 2))
                    stand_alone(dve)
                    for j in range(2):
                        nc.vector.bn_aggr(mv2[:, j, :], st2[:, j, :]).then_inc(stats2, 1)
                if A:
                    maximum(1)
                if C:
                    low_part(2)
                if A:
                    maximum(2)
                if C:
                    low_part(3)
                if A:
                    maximum(3)
                if L:
                    dve.wait_ge(x_in[nl.par], nl.at2(DMA))
                    if not (isinstance(nl.i, int) and nl.k < 1):
                        dve.wait_ge(scale1, (nl + -1).at(4, 4))
                    stand_alone(dve)
                    for j in range(2):
                        nc.vector.bn_stats(st1[:, j, :], X[:, bass.ds(nl.index() * 2 + j, 1), :].rearrange("p a c -> p (a c)")).then_inc(ln1_step, 1)
                    dve.wait_ge(ln1_step, nl.at(2, 2))
                    stand_alone(dve)
                    for j in range(2):
                        nc.vector.bn_aggr(mv1[:, j, :], st1[:, j, :]).then_inc(stats1, 1)
                if C:
                    low_part(4)
                if D_:
                    dve.wait_ge(hr_ready, d.at(1, 1))
                    nc.vector.tensor_copy(logits[:, bass.ds(d.index() * 2, 2), :],
                                          M1[:, 0:2 * (F + NE)].rearrange("p (j f) -> p j f", j=2)[:, :, F:F + NE]).then_inc(logits_ready, 1)
                if C:
                    low_part(5)
                if D_:
                    dve.wait_ge(ffn_done, d.at(1, 1))
                    if not (isinstance(d.i, int) and d.k < 2):
                        dve.wait_ge(out_stored[d.par], (d + -2).at2(DMA))
                    nc.vector.tensor_tensor(ost[:, d.par, :, :], M1[:, :].rearrange("p (j c) -> p j c", j=2),
                                            X[:, bass.ds(d.index() * 2, 2), :], ALU.add).then_inc(out_ready, 1)

            schedule(dve, step)
            k = [0]

            def link(ins):
                k[0] += 1
                ins.then_inc(top_step, 1)
                dve.wait_ge(top_step, k[0])

            dve.wait_ge(logits_ready, NB)
            first, second, gap, e_gap, many = (top[:, n, :] for n in range(5))
            wide = lambda t: t.unsqueeze(2).to_broadcast([P, NT, NE])
            link(nc.vector.tensor_reduce(first, logits[:, :, :], AX.X, ALU.max))
            link(nc.vector.tensor_tensor(prob[:, :, :], logits[:, :, :], wide(first), ALU.is_ge))
            link(nc.vector.tensor_reduce(many, prob[:, :, :], AX.X, ALU.add))
            link(nc.vector.scalar_tensor_tensor(l2[:, :, :], prob[:, :, :], -BIG, logits[:, :, :], ALU.mult, ALU.add))
            link(nc.vector.tensor_reduce(second, l2[:, :, :], AX.X, ALU.max))
            link(nc.vector.tensor_tensor(gap, second, first, ALU.subtract))
            dve.wait_ge(gap_exp, 1)
            link(nc.vector.tensor_scalar(second, e_gap, 1.0, None, ALU.add))
            link(nc.vector.reciprocal(first, second))
            link(nc.vector.tensor_scalar(gap, first, 1.0, None, ALU.is_ge))
            link(nc.vector.scalar_tensor_tensor(first, many, 1.0, gap, ALU.is_equal, ALU.mult))
            link(nc.vector.tensor_tensor(prob[:, :, :], prob[:, :, :], wide(first), ALU.mult))
            link(nc.vector.tensor_reduce(any1[:, :], prob[:, :, :].rearrange("p n e -> p (n e)"), AX.X, ALU.max))
            dve.wait_ge(any_done, 1)
            nc.vector.tensor_copy(flag[0:1, 0:1], M0[0:1, 0:1]).then_inc(flag_ready, 1)
            dve.wait_ge(flag_ready, 1)
            with dve.If(dve.value_load(flag[0:1, 0:1]) != 0):
                dve.sem_inc(g_added, 1)
                with dve.Fori(0, NT) as t:
                    dve.wait_ge(g_added, t * NE + 1)
                    stand_alone(dve)
                    nc.vector.bn_stats(st2[:, 0, :], X[:, bass.ds(t, 1), :].rearrange("p a c -> p (a c)")).then_inc(g_step, 1)
                    dve.wait_ge(g_step, t + 1)
                    stand_alone(dve)
                    nc.vector.bn_aggr(mv2[:, 0, :], st2[:, 0, :]).then_inc(g_stats, 1)
                    dve.wait_ge(g_out_in, t * DMA + DMA)
                    for e in range(NE):
                        dve.wait_ge(g_y, t * NE + (e + 1))
                        dve.wait_ge(g_added, t * NE + (e + 1))
                        nc.vector.scalar_tensor_tensor(gout[:, :], psS[0][:, 0:D],
                                                       prob[:, bass.ds(t, 1), e:e + 1].rearrange("p n e -> p (n e)"),
                                                       gout[:, :], ALU.mult, ALU.add).then_inc(g_added, 1)

        @block.tensor
        def _(pe):
            pe.wait_ge(consts_in, 2 * DMA)
            for c in range(NKC):
                for h in range(2):
                    if c >= 1:
                        pe.wait_ge(ktl_ready, 2 * (c - 1) + h + 1)
                    nc.tensor.matmul(psA[:, 512 * h:512 * h + KC], wk[:, h * P:(h + 1) * P],
                                     z[:, KB * c:KB * (c + 1), :], start=True, stop=True).then_inc(kproj, 1)
            pe.wait_ge(const1_in, NCONST * DMA)
            pe.wait_ge(ktl_ready, 2 * NKC)

            def step(b, L, A, C, D_):
                na, d = b + 1, b + -1
                past = not isinstance(b.i, int)

                def scores(j):
                    s0, n = GROUPS[j]
                    e = (6 * b.par + j) % 2
                    if j == 0:
                        pe.wait_ge(kst_in[b.par], b.at2(4 * DMA))
                        pe.wait_ge(qst_in[b.par], b.at2(2 * DMA))
                        pe.wait_ge(m_in[b.par], b.at2(DMA))
                    if past or 6 * b.k + j >= 2:
                        pe.wait_ge(ph_ready, b.at(6, j - 1))
                    for u in range(n):
                        last = nc.tensor.matmul(psS[e][:, u * S:(u + 1) * S], kst[:, b.par, s0 + u, :],
                                                qst[:, b.par, s0 + u, :], start=True, stop=True)
                    last.then_inc(s_done, 1)

                def values(j):
                    s0, n = GROUPS[j]
                    e = (6 * b.par + j) % 2
                    if j == 0:
                        pe.wait_ge(v_ready, b.at(4, 4))
                        if past or b.k >= 1:
                            pe.wait_ge(on_ready, d.at(2, 2))
                    pe.wait_ge(pl_ready, b.at(6, j + 1))
                    for t in range(2):
                        for u in range(n):
                            s = s0 + u
                            nh, h0, blk = NHS[s], FIRST[s], VBLK[s]
                            o = psO[t][:, h0 * OC:(h0 + nh) * OC]
                            q = slice(t * P, (t + 1) * P)
                            for m, (p_, v_) in enumerate(((ph, v1), (ph, v2), (ph, v3), (pl, v1), (pl, v2))):
                                last = nc.tensor.matmul(o, p_[:, e, u, q],
                                                        v_[:, b.par, blk:blk + nh, :].rearrange("p n c -> p (n c)"),
                                                        start=(s == 0 and m == 0), stop=(s == NSL - 1 and m == 4),
                                                        skip_group_check=True)
                    last.then_inc(pv_done, 1)

                def maxima_scores(j):
                    t, h = j // 2, j % 2
                    if j == 0:
                        pe.wait_ge(kbd_ready, na.at(2, 2))
                        pe.wait_ge(qh_ready, na.at(1, 1))
                    if past or 4 * na.k + j >= 1:
                        pe.wait_ge(max_ready, na.at(4, j))
                    for u in range(2):
                        last = nc.tensor.matmul(psA[:, 512 * u:512 * u + HG], qh[:, na.par, h, t * P:(t + 1) * P],
                                                kbd[:, na.par, h, u * HG:(u + 1) * HG], start=True, stop=True)
                    last.then_inc(sa_done, 1)

                def transposes(dst, src, done):
                    for k in range(2):
                        for t in range(2):
                            last = nc.tensor.transpose(dst[:, k * S + t * P:k * S + (t + 1) * P],
                                                       src[:, t, k * P:(k + 1) * P], ident[:, :])
                    last.then_inc(done, 1)

                if A:
                    if past or b.k >= 2:
                        pe.wait_ge(hT_ready, (b + -2).at(1, 1))
                    elif b.k >= 0:
                        pe.wait_ge(mh_ready, b.at(1, 1))
                    na_cols = 11 * HD
                    pe.wait_ge(zc_in[na.par], na.at2(DMA))
                    nc.tensor.matmul(M0[:, 0:na_cols], zc[:, na.par, 0:P], wv[:, 0:na_cols], start=True, stop=True)
                    nc.tensor.matmul(M0[:, na_cols:NBLK * HD], zc[:, na.par, CUT:CUT + P], wv[:, na_cols:NBLK * HD],
                                     start=True, stop=True).then_inc(v_done, 1)
                    if past or b.k >= 2:
                        pe.wait_ge(out_ready, (b + -2).at(1, 1))
                    elif b.k >= 0:
                        pe.wait_ge(ql_ready, b.at(1, 1))
                    pe.wait_ge(xn_ready, na.at(1, 1))
                    transposes(M1, xn[:, na.par, :, :], xT_done)
                if C:
                    scores(0)
                if D_:
                    if A:
                        pe.wait_ge(v_masked, na.at(1, 1))
                    else:
                        pe.wait_ge(hT_ready, (d + -1).at(1, 1))
                    pe.wait_ge(on_ready, d.at(2, 2))
                    transposes(M0, on[:, :, :], oT_done)
                if A:
                    pe.wait_ge(xnT_ready, na.at(1, 1))
                    for h in range(2):
                        for k in range(2):
                            last = nc.tensor.matmul(M1[:, h * S:(h + 1) * S], wq[:, k, h * P:(h + 1) * P], xnT[:, k, :],
                                                    start=(k == 0), stop=(k == 1))
                    last.then_inc(q_done, 1)
                if C:
                    scores(1)
                    values(0)
                if A:
                    maxima_scores(0)
                if D_:
                    pe.wait_ge(onT_ready, d.at(1, 1))
                    for t in range(2):
                        for k in range(2):
                            last = nc.tensor.matmul(M0[:, t * D:(t + 1) * D], onT[:, k, t * P:(t + 1) * P], wo[:, k, :],
                                                    start=(k == 0), stop=(k == 1))
                    last.then_inc(attn_done, 1)
                if C:
                    scores(2)
                if A:
                    maxima_scores(1)
                if C:
                    values(1)
                if A:
                    maxima_scores(2)
                if C:
                    scores(3)
                    values(2)
                if D_:
                    if A:
                        pe.wait_ge(ql_ready, na.at(1, 1))
                    else:
                        pe.wait_ge(out_ready, (d + -1).at(1, 1))
                    pe.wait_ge(yn_ready, d.at(1, 1))
                    transposes(M1, yn[:, :, :], yT_done)
                if A:
                    maxima_scores(3)
                    if D_:
                        pe.wait_ge(y_ready, d.at(1, 1))
                    else:
                        pe.wait_ge(v_masked, na.at(1, 1))
                    pe.wait_ge(max_ready, na.at(4, 4))
                    for t in range(2):
                        last = nc.tensor.transpose(M0[0:H, t * P:(t + 1) * P], nm[:, t, :], ident[:, :])
                    last.then_inc(mT_done, 1)
                if C:
                    scores(4)
                    values(3)
                if D_:
                    pe.wait_ge(ynT_ready, d.at(1, 1))
                    for t in range(2):
                        for k in range(2):
                            last = nc.tensor.matmul(M1[:, t * (F + NE):(t + 1) * (F + NE)], ynT[:, k, t * P:(t + 1) * P],
                                                    w1r[:, k, :], start=(k == 0), stop=(k == 1))
                    last.then_inc(h_done, 1)
                if C:
                    scores(5)
                    values(4)
                if D_:
                    if A:
                        pe.wait_ge(mh_ready, na.at(1, 1))
                    else:
                        pe.wait_ge(y_ready, d.at(1, 1))
                    pe.wait_ge(hr_ready, d.at(1, 1))
                    for t in range(2):
                        last = nc.tensor.transpose(M0[:, t * P:(t + 1) * P], hr[:, t, :], ident[:, :])
                    last.then_inc(hT_done, 1)
                if C:
                    values(5)
                if D_:
                    pe.wait_ge(logits_ready, d.at(1, 1))
                    pe.wait_ge(hT_ready, d.at(1, 1))
                    for t in range(2):
                        last = nc.tensor.matmul(M1[:, t * D:(t + 1) * D], hT[:, t * P:(t + 1) * P], ws2[:, :],
                                                start=True, stop=True)
                    last.then_inc(ffn_done, 1)

            schedule(pe, step)
            pe.wait_ge(top_step, 12)
            pe.wait_ge(hT_ready, NB)
            nc.tensor.matmul(M0[0:1, 0:1], any1[:, :], ones[:, :], start=True, stop=True).then_inc(any_done, 1)
            pe.wait_ge(flag_ready, 1)
            with pe.If(pe.value_load(flag[0:1, 0:1]) != 0):
                pe.wait_ge(experts_in, 2 * DMA)
                with pe.Fori(0, NT) as t:
                    pe.wait_ge(g_yn, t + 1)
                    for k in range(2):
                        last = nc.tensor.transpose(M0[:, k * P:(k + 1) * P], yn[:, 0, k * P:(k + 1) * P], ident[:, :])
                    last.then_inc(g_yT, 1)
                    pe.wait_ge(g_ynT, t + 1)
                    for e in range(NE):
                        pe.wait_ge(g_hT, t * NE + (e + 1))
                        for k in range(2):
                            last = nc.tensor.matmul(M1[:, 0:P], w1[:, k, e, :], ynT[:, k, 0:P], start=(k == 0), stop=(k == 1))
                        last.then_inc(g_h, 1)
                        pe.wait_ge(g_hT, t * NE + (e + 2))
                        pe.wait_ge(g_added, t * NE + (e + 1))
                        nc.tensor.matmul(psS[0][:, 0:D], hT[:, 0:P], w2[:, e, :], start=True, stop=True).then_inc(g_y, 1)


def kernel(x, ctx_512, L0_xattn_Wq, L0_xattn_Wkv, L0_xattn_Wo, L0_ffn_Ws1, L0_ffn_Ws2, L0_ffn_W1, L0_ffn_W2,
           L0_ffn_Wr):
    import numpy as np
    import concourse.bacc as bacc
    from concourse.bass_utils import run_bass_kernel_spmd

    f32 = np.float32
    cols = lambda w: w.reshape(2, P, -1).transpose(1, 0, 2)
    zt = ctx_512.transpose(2, 0, 1)
    wvt = L0_xattn_Wkv[D:].T.reshape(LAT, H, HD)
    order = [h for i in range(6) for h in (3 * i, 3 * i + 1) if h < H] + [h for i in range(5) for h in (3 * i + 1, 3 * i + 2)]
    row = np.arange(P)
    mask = np.zeros((P, NBLK), f32)
    sel = np.zeros((2, H, NSL, P), f32)
    for s in range(NSL):
        spans = ((0, NK), (NK, P)) if s % 2 == 0 else ((0, REST), (REST, REST + NK))
        for n in range(NHS[s]):
            own = (row >= spans[n][0]) & (row < spans[n][1])
            mask[:, VBLK[s] + n] = own
            sel[0, FIRST[s] + n, s, :] = own
    arrays = {
        "x": x.reshape(NB * S, D),
        "z": zt,
        "zz": np.concatenate([zt, zt, zt[:, :, :REST]], axis=2),
        "wq": cols(L0_xattn_Wq.T),
        "wk": L0_xattn_Wkv[:D].T,
        "wv": wvt[:, order, :].reshape(LAT, NBLK * HD),
        "wo": cols(L0_xattn_Wo.T),
        "w1r": cols(np.concatenate([L0_ffn_Ws1, L0_ffn_Wr], axis=1)),
        "ws2": L0_ffn_Ws2,
        "w1": L0_ffn_W1.reshape(NE, 2, P, F).transpose(2, 1, 0, 3),
        "w2": L0_ffn_W2.transpose(1, 0, 2),
        "ident": np.eye(P, dtype=f32),
        "mask": mask,
        "headmask": (row[:, None] // HD == np.arange(8)).astype(f32),
        "sel": sel.reshape(32, NSL * P),
    }
    arrays = {n: np.ascontiguousarray(a) for n, a in arrays.items()}
    nc = bacc.Bacc("TRN2", target_bir_lowering=False, num_devices=1)
    args = [nc.dram_tensor(f"in_{n}", a.shape, FP32, kind="ExternalInput").ap() for n, a in arrays.items()]
    out = nc.dram_tensor("out", (NB * S, D), FP32, kind="ExternalOutput").ap()
    build(nc, *args, out)
    r = run_bass_kernel_spmd(nc, [{f"in_{n}": a for n, a in arrays.items()}], core_ids=[0])
    return r.results[0]["out"].reshape(NB, S, D)
```

```python
import concourse.bass as bass
from concourse import mybir
from concourse.alu_op_type import AluOpType as ALU
from contextlib import ExitStack

FP32 = mybir.dt.float32
FP32R = mybir.dt.float32r
BF16 = mybir.dt.bfloat16
FP16 = mybir.dt.float16
I32 = mybir.dt.int32
ACT = mybir.ActivationFunctionType
AX = mybir.AxisListType

P = 128
NB, S, D = 32, 256, 256
NT = NB * S // P
LAT, NK = 128, 77
H, HD = 16, 16
F, NE = 128, 8
EPS = 1e-5
SCALE = HD ** -0.5
BIG = 3.0e38

PARTS = 3
HR = PARTS * HD
MROW = 2 * HR
CUT = P - NK
REST = NK - CUT
ZW = 2 * NK + REST
NSL = 11
FIRST = [3 * (s // 2) + s % 2 for s in range(NSL)]
NHS = [min(2, H - f) for f in FIRST]
VBLK = [2 * (s // 2) if s % 2 == 0 else 11 + 2 * (s // 2) for s in range(NSL)]
NBLK = 21
GROUPS = [(2 * j, min(2, NSL - 2 * j)) for j in range(6)]
NCONST = 9
OC = HD + 1
HG = 4 * NK
KB = 4
NKC = NB // KB
KC = KB * NK
DMA = 16


class Batch:

    def __init__(self, i, k):
        self.i, self.k = i, k

    def __add__(self, d):
        return Batch(self.i, self.k + d)

    def __sub__(self, d):
        return Batch(self.i, self.k - d)

    @property
    def exists(self):
        return not isinstance(self.i, int) or 0 <= self.k < NB

    @property
    def par(self):
        return self.k % 2

    def at(self, per, j):
        return self.i * (2 * per) + (self.k * per + j)

    def at2(self, per):
        return self.i * per + (self.k // 2 + 1) * per

    def index(self):
        return self.i * 2 + self.k


LOOP_FROM, LOOP_TO = 6, 28


def schedule(eng, step):
    def call(s):
        step(*(s + n for n in (3, 2, 1, 0, -1, -2, -3)))
    for s in range(-3, LOOP_FROM):
        call(Batch(0, s))
    with eng.Fori(LOOP_FROM // 2, LOOP_TO // 2) as i:
        call(Batch(i, 0))
        call(Batch(i, 1))
    for s in range(LOOP_TO, NB + 3):
        call(Batch(0, s))


def build(nc, x_d, z_d, zz_d, wq_d, wk_d, wv_d, wo_d, w1r_d, ws2_d, w1_d, w2_d, ident_d, mask_d, headmask_d, sel_d, out_d):
    kt_d = nc.dram_tensor("kt_scratch", (2 * P, PARTS, NB * NK), FP32, kind="Internal").ap()
    qt_d = nc.dram_tensor("qt_scratch", (2, (H + 2) * HD, PARTS, S), FP32, kind="Internal").ap()
    ctx = ExitStack()
    with ctx:
        def sb(name, shape, dt=FP32):
            return ctx.enter_context(nc.sbuf_tensor(name, shape, dt))

        def sem(name):
            return ctx.enter_context(nc.semaphore(name))

        def sem2(name):
            return [sem(f"{name}{p}") for p in range(2)]

        X = sb("X", [P, NT, D])
        zw = sb("zw", [P, 2 * NE * F + NE * D])
        z = zw[:, 0:NB * NK].rearrange("p (b k) -> p b k", k=NK)
        sel = zw[:, NB * NK:NB * NK + NSL * P]
        w1 = zw[:, 0:2 * NE * F].rearrange("p (k e f) -> p k e f", k=2, e=NE)
        w2 = zw[:, 2 * NE * F:].rearrange("p (e d) -> p e d", e=NE)
        zc = sb("zc", [P, 2, ZW])
        wq = sb("wq", [P, 2, D])
        wk = sb("wk", [P, D])
        wv = sb("wv", [P, NBLK * HD])
        wo = sb("wo", [P, 2, D])
        w1r = sb("w1r", [P, 2, F + NE])
        ws2 = sb("ws2", [P, D])
        ident = sb("ident", [P, P])
        mask = sb("mask", [P, NBLK])
        kth = sb("kth", [P, 2, 2, KC], FP32R)
        ktl = sb("ktl", [P, 2, 2, KC], FP32R)
        kT = sb("kT", [P, 2, 2, NK])
        headmask = sb("headmask", [P, 8])
        kbd = sb("kbd", [P, 2, 2, 8 * NK], FP32R)
        kst = sb("kst", [P, 2, NSL, P], FP32R)
        qst = sb("qst", [P, 2, NSL, S], FP32R)
        st1 = sb("st1", [P, 2, 6])
        mv1 = sb("mv1", [P, 2, 2])
        ve1 = sb("ve1", [P, 2])
        rs1 = sb("rs1", [P, 2])
        nb1 = sb("nb1", [P, 2])
        st2 = sb("st2", [P, 2, 6])
        mv2 = sb("mv2", [P, 2, 2])
        ve2 = sb("ve2", [P, 2])
        rs2 = sb("rs2", [P, 2])
        nb2 = sb("nb2", [P, 2])
        mhalf = sb("mhalf", [P, 2])
        xn = sb("xn", [P, 2, 2, D])
        xnT = sb("xnT", [P, 2, S])
        qh = sb("qh", [P, 2, 2, S], FP32R)
        ql = sb("ql", [P, 2, 2, S], FP32R)
        nm = sb("nm", [P, 2, H])
        mh = sb("mh", [H, S], FP32R)
        vf = sb("vf", [P, NBLK, HD])
        vr = sb("vr", [P, NBLK, HD])
        v1 = sb("v1", [P, 2, NBLK, OC], BF16)
        v2 = sb("v2", [P, 2, NBLK, OC], BF16)
        v3 = sb("v3", [P, 2, NBLK, OC], BF16)
        E = sb("E", [P, 2, 2, S])
        ph = sb("ph", [P, 2, 2, S], FP16)
        pl = sb("pl", [P, 2, 2, S], FP16)
        rden = sb("rden", [P, 2, H])
        on = sb("on", [P, 2, D])
        onT = sb("onT", [P, 2, S])
        yn = sb("yn", [P, 2, D])
        ynT = sb("ynT", [P, 2, S])
        hr = sb("hr", [P, 2, F])
        hT = sb("hT", [P, S])
        ost = sb("ost", [P, 2, 2, D])
        logits = sb("logits", [P, NT, NE])
        prob = sb("prob", [P, NT, NE])
        top = sb("top", [P, 5, NT])
        ones = sb("ones", [P, 1])
        any1 = sb("any1", [P, 1])
        flag = sb("flag", [1, 1], I32)
        l2 = sb("l2", [P, NT, NE])
        gout = sb("gout", [P, D])

        def pb(name, cols):
            return ctx.enter_context(nc.psum_tensor(name, [P, cols], FP32))

        psS = [pb(f"psS{j}", 512) for j in range(2)]
        psO = [pb(f"psO{j}", 512) for j in range(2)]
        psA = pb("psA", 1024)
        M0, M1 = pb("M0", 512), pb("M1", 512)

        consts_in = sem("consts_in")
        const1_in = sem("const1_in")
        experts_in = sem("experts_in")
        x_in = sem2("x_in")
        zc_in = sem2("zc_in")
        kT_in = sem2("kT_in")
        qt_stored = sem2("qt_stored")
        pad_stored = sem("pad_stored")
        kbd_ready = sem("kbd_ready")
        kst_in = sem2("kst_in")
        qst_in = sem2("qst_in")
        m_in = sem2("m_in")
        out_stored = sem2("out_stored")
        kt_stored = sem2("kt_stored")
        zeroed = sem("zeroed")
        kst_ready = sem("kst_ready")
        kproj, kth_ready, ktl_ready = sem("kproj"), sem("kth_ready"), sem("ktl_ready")
        stats1, scale1, xn_ready = sem("stats1"), sem("scale1"), sem("xn_ready")
        v_done, v_masked, v_ready = sem("v_done"), sem("v_masked"), sem("v_ready")
        pool_step = sem("pool_step")
        ln1_step, ln2_step = sem("ln1_step"), sem("ln2_step")
        xT_done, xnT_ready = sem("xT_done"), sem("xnT_ready")
        q_done, qh_ready, ql_ready = sem("q_done"), sem("qh_ready"), sem("ql_ready")
        sa_done, max_ready = sem("sa_done"), sem("max_ready")
        mT_done, mh_ready = sem("mT_done"), sem("mh_ready")
        s_done, e_ready, ph_ready, pl_ready = sem("s_done"), sem("e_ready"), sem("ph_ready"), sem("pl_ready")
        pv_done, den_ready, on_ready = sem("pv_done"), sem("den_ready"), sem("on_ready")
        oT_done, onT_ready = sem("oT_done"), sem("onT_ready")
        attn_done, y_ready = sem("attn_done"), sem("y_ready")
        stats2, scale2, yn_ready = sem("stats2"), sem("scale2"), sem("yn_ready")
        yT_done, ynT_ready = sem("yT_done"), sem("ynT_ready")
        h_done, hr_ready, logits_ready = sem("h_done"), sem("hr_ready"), sem("logits_ready")
        hT_done, hT_ready = sem("hT_done"), sem("hT_ready")
        ffn_done, out_ready = sem("ffn_done"), sem("out_ready")
        top_step, gap_exp, any_done, flag_ready = sem("top_step"), sem("gap_exp"), sem("any_done"), sem("flag_ready")
        E_ = mybir.EngineType
        passed = {e: sem(f"passed_{e.name}") for e in (E_.SP, E_.DVE, E_.Pool)}
        g_out_in, g_stored, g_added = sem("g_out_in"), sem("g_stored"), sem("g_added")
        g_step, g_stats, g_scale, g_yn = sem("g_step"), sem("g_stats"), sem("g_scale"), sem("g_yn")
        g_yT, g_ynT, g_h, g_relu = sem("g_yT"), sem("g_ynT"), sem("g_h"), sem("g_relu")
        g_hT, g_y = sem("g_hT"), sem("g_y")

        def stand_alone(eng):
            eng.sem_inc(passed[eng.engine], 1)

        x_t = x_d.rearrange("(n j p) d -> p n j d", p=P, j=2)
        out_t = out_d.rearrange("(n j p) d -> p n j d", p=P, j=2)

        block = ctx.enter_context(nc.Block())

        @block.sync
        def _(sp):
            sp.dma_start(z[:, :, :], z_d).then_inc(consts_in, DMA)
            sp.dma_start(wk[:, :], wk_d).then_inc(consts_in, DMA)
            for b in range(2):
                sp.dma_start(X[:, 2 * b:2 * b + 2, :], x_t[:, b]).then_inc(x_in[b], DMA)
                sp.dma_start(zc[:, b, :], zz_d[:, b, :]).then_inc(zc_in[b], DMA)
            for dst, src in ((sel[MROW:P, :], sel_d), (mask[:, :], mask_d), (headmask[:, :], headmask_d), (ident[:, :], ident_d),
                             (wq[:, :, :], wq_d), (wv[:, :], wv_d), (wo[:, :, :], wo_d),
                             (w1r[:, :, :], w1r_d), (ws2[:, :], ws2_d)):
                sp.dma_start(dst, src).then_inc(const1_in, DMA)
            for c in range(NKC):
                p = c % 2
                cols = slice(c * KC, (c + 1) * KC)
                if c >= 2:
                    sp.wait_ge(kt_stored[p], PARTS * DMA * (c // 2))
                dst = kt_d[:, :, cols].rearrange("(h p) n c -> p h n c", p=P)
                sp.wait_ge(kth_ready, 2 * (c + 1))
                for n in range(2):
                    sp.dma_start(dst[:, :, n, :], kth[:, p, :, :].bitcast(FP32)).then_inc(kt_stored[p], DMA)
                sp.wait_ge(ktl_ready, 2 * (c + 1))
                sp.dma_start(dst[:, :, 2, :], ktl[:, p, :, :].bitcast(FP32)).then_inc(kt_stored[p], DMA)
            sp.wait_ge(zeroed, 4)
            for p in range(2):
                sp.dma_start(qt_d[p, H * HD:(H + 1) * HD].rearrange("r n q -> (r n) q"),
                             qst[0:HR, p, 0, :].bitcast(FP32)).then_inc(pad_stored, DMA)
            for p in range(2):
                sp.wait_ge(kt_stored[p], PARTS * DMA * (NKC // 2))
            sp.wait_ge(pad_stored, 2 * DMA)
            sp.wait_ge(kst_ready, 2)

            kt_rows = kt_d.rearrange("r n (b k) -> (r n) b k", k=NK).rearrange("(i r) b k -> r i b k", r=HR)
            kt_high = kt_d[:, 0, :].rearrange("(h p) (b k) -> p h b k", p=P, k=NK)

            def load_kT(b):
                sp.dma_start(kT[:, b.par, :, :], kt_high[:, :, bass.ds(b.index(), 1), :].rearrange("p h b k -> p h (b k)")
                             ).then_inc(kT_in[b.par], DMA)

            def load_kst(b):
                roles = ((0, 0, 6, 0, 0, NK, 0), (1, 0, 5, HR, NK, P, 0),
                         (1, 1, 5, 0, 0, REST, CUT), (2, 1, 5, HR, REST, REST + NK, 0))
                for head, first, n, r, c0, c1, k0 in roles:
                    src = kt_rows[:, head:head + 3 * (n - 1) + 1:3, bass.ds(b.index(), 1), k0:k0 + c1 - c0]
                    sp.dma_start(kst[r:r + HR, b.par, first:first + 2 * (n - 1) + 1:2, c0:c1].bitcast(FP32),
                                 src.rearrange("r i b k -> r i (b k)")).then_inc(kst_in[b.par], DMA)

            def store_q(b, part, n):
                sp.dma_start(qt_d[b.par, 0:H * HD, n, :].rearrange("(h p) q -> p h q", p=P),
                             part[:, b.par, :, :].bitcast(FP32)).then_inc(qt_stored[b.par], DMA)

            def stack_q(b):
                src = qt_d[b.par].rearrange("r n q -> (r n) q").rearrange("(i r) q -> r i q", r=3 * HR)
                sp.dma_start(qst[0:2 * HR, b.par, 0:NSL:2, :].bitcast(FP32), src[0:2 * HR]).then_inc(qst_in[b.par], DMA)
                sp.dma_start(qst[0:2 * HR, b.par, 1:NSL:2, :].bitcast(FP32), src[HR:3 * HR, 0:5]).then_inc(qst_in[b.par], DMA)

            def step(l, a, m, c, d, f, g):
                if m.exists:
                    if (c - 1).exists:
                        sp.wait_ge(s_done, (c - 1).at(6, 6))
                        stand_alone(sp)
                        sp.wait_ge(kst_in[m.par], (m - 2).at2(4 * DMA))
                        stand_alone(sp)
                        sp.wait_ge(m_in[m.par], (m - 2).at2(DMA))
                        stand_alone(sp)
                    load_kst(m)
                    sp.wait_ge(qt_stored[m.par], m.at2(PARTS * DMA))
                    stand_alone(sp)
                    stack_q(m)
                if l.exists:
                    if (l - 2).exists:
                        sp.wait_ge(x_in[l.par], (l - 2).at2(DMA))
                        stand_alone(sp)
                        sp.dma_start(X[:, bass.ds(l.index() * 2, 2), :],
                                     x_t[:, bass.ds(l.index(), 1)].rearrange("p n j d -> p (n j) d")
                                     ).then_inc(x_in[l.par], DMA)
                        sp.wait_ge(kbd_ready, (l - 2).at(2, 2))
                        stand_alone(sp)
                    load_kT(l)
                if a.exists and (a - 2).exists:
                    sp.wait_ge(v_done, (a - 2).at(1, 1))
                    stand_alone(sp)
                    sp.dma_start(zc[:, a.par, :], zz_d[:, bass.ds(a.index(), 1), :].rearrange("p b c -> p (b c)")
                                 ).then_inc(zc_in[a.par], DMA)
                if g.exists:
                    sp.wait_ge(out_ready, g.at(1, 1))
                    stand_alone(sp)
                    sp.dma_start(out_t[:, bass.ds(g.index(), 1)].rearrange("p n j d -> p (n j) d"),
                                 ost[:, g.par, :, :]).then_inc(out_stored[g.par], DMA)
                if a.exists:
                    sp.wait_ge(qh_ready, a.at(1, 1))
                    stand_alone(sp)
                    store_q(a, qh, 0)
                    store_q(a, qh, 2)
                    sp.wait_ge(ql_ready, a.at(1, 1))
                    stand_alone(sp)
                    store_q(a, ql, 1)
                if m.exists:
                    sp.wait_ge(mh_ready, m.at(1, 1))
                    stand_alone(sp)
                    sp.dma_start(qst[MROW:MROW + H, m.par, :, :].bitcast(FP32),
                                 mh[:, :].bitcast(FP32).unsqueeze(1).to_broadcast([H, NSL, S])).then_inc(m_in[m.par], DMA)

            schedule(sp, step)
            for p in range(2):
                sp.wait_ge(out_stored[p], DMA * NB // 2)
            sp.wait_ge(flag_ready, 1)
            with sp.If(sp.value_load(flag[0:1, 0:1]) != 0):
                sp.dma_start(w1[:, :, :, :], w1_d).then_inc(experts_in, DMA)
                sp.dma_start(w2[:, :, :], w2_d).then_inc(experts_in, DMA)
                out_n = out_d.rearrange("(n p) d -> p n d", p=P)
                sp.sem_inc(g_stored, DMA)
                with sp.Fori(0, NT) as t:
                    sp.wait_ge(g_stored, t * DMA + DMA)
                    stand_alone(sp)
                    sp.dma_start(gout[:, :], out_n[:, bass.ds(t, 1), :].rearrange("p n d -> p (n d)")).then_inc(g_out_in, DMA)
                    sp.wait_ge(g_added, t * NE + (NE + 1))
                    stand_alone(sp)
                    sp.dma_start(out_n[:, bass.ds(t, 1), :].rearrange("p n d -> p (n d)"), gout[:, :]).then_inc(g_stored, DMA)
                sp.wait_ge(g_stored, NT * DMA + DMA)

        @block.gpsimd
        def _(pool):
            for t in (qst, kst):
                nc.gpsimd.memset(t[:, 0].bitcast(FP32), 0.0).then_inc(zeroed, 1)
                nc.gpsimd.memset(t[:, 1].bitcast(FP32), 0.0).then_inc(zeroed, 1)
            nc.gpsimd.memset(mhalf[:, :], -0.5).then_inc(pool_step, 1)
            nc.gpsimd.memset(ones[:, :], 1.0).then_inc(pool_step, 1)
            nc.gpsimd.memset(v2[:, :, :, :], 0.0).then_inc(pool_step, 1)
            nc.gpsimd.memset(v3[:, :, :, :], 0.0).then_inc(pool_step, 1)
            pool.wait_ge(const1_in, NCONST * DMA)
            for p in range(2):
                nc.gpsimd.tensor_copy(v1[:, p, :, HD:OC], mask[:, :].unsqueeze(2)).then_inc(pool_step, 1)
            pool.wait_ge(pool_step, 6)

            def rsqrt(stats, scale, mv, ve, rs, nb, bt):
                pool.wait_ge(stats, bt.at(2, 2))
                if (bt - 1).exists:
                    pool.wait_ge(xn_ready if scale is scale1 else yn_ready, (bt - 1).at(1, 1))
                stand_alone(pool)
                nc.gpsimd.tensor_scalar(ve[:, :], mv[:, :, 1], EPS, 1.0, ALU.add, ALU.mult).then_inc(scale, 1)
                pool.wait_ge(scale, bt.at(4, 1))
                nc.gpsimd.tensor_tensor(rs[:, :], ve[:, :], mhalf[:, :], ALU.pow).then_inc(scale, 1)
                pool.wait_ge(scale, bt.at(4, 2))
                stand_alone(pool)
                for j in range(2):
                    nc.gpsimd.tensor_scalar(nb[:, j:j + 1], rs[:, j:j + 1], mv[:, j, 0:1], -1.0,
                                            ALU.mult, ALU.mult).then_inc(scale, 1)

            def split_v(b):
                pool.wait_ge(v_masked, b.at(1, 1))
                if (b - 2).exists:
                    pool.wait_ge(pv_done, (b - 2).at(6, 6))
                stand_alone(pool)
                p = b.par
                nc.gpsimd.tensor_copy(v1[:, p, :, 0:HD], vf[:, :, :]).then_inc(v_ready, 1)
                pool.wait_ge(v_ready, b.at(4, 1))
                nc.gpsimd.tensor_tensor(vr[:, :, :], vf[:, :, :], v1[:, p, :, 0:HD], ALU.subtract).then_inc(v_ready, 1)
                pool.wait_ge(v_ready, b.at(4, 2))
                stand_alone(pool)
                nc.gpsimd.tensor_copy(v2[:, p, :, 0:HD], vr[:, :, :]).then_inc(v_ready, 1)
                pool.wait_ge(v_ready, b.at(4, 3))
                nc.gpsimd.tensor_tensor(v3[:, p, :, 0:HD], vr[:, :, :], v2[:, p, :, 0:HD], ALU.subtract).then_inc(v_ready, 1)

            def diagonal_keys(b):
                pool.wait_ge(kT_in[b.par], b.at2(DMA))
                stand_alone(pool)
                if (b - 2).exists:
                    pool.wait_ge(sa_done, (b - 2).at(4, 4))
                    stand_alone(pool)
                for h in range(2):
                    nc.gpsimd.tensor_tensor(kbd[:, b.par, h, :].rearrange("p (h k) -> p h k", k=NK),
                                            kT[:, b.par, h, :].unsqueeze(1).to_broadcast([P, 8, NK]),
                                            headmask[:, :].unsqueeze(2).to_broadcast([P, 8, NK]), ALU.mult).then_inc(kbd_ready, 1)

            def step(l, a, m, c, d, f, g):
                if f.exists:
                    rsqrt(stats2, scale2, mv2, ve2, rs2, nb2, f)
                if m.exists:
                    split_v(m)
                if l.exists:
                    rsqrt(stats1, scale1, mv1, ve1, rs1, nb1, l)
                if a.exists:
                    diagonal_keys(a)

            schedule(pool, step)
            pool.wait_ge(flag_ready, 1)
            with pool.If(pool.value_load(flag[0:1, 0:1]) != 0):
                with pool.Fori(0, NT) as t:
                    pool.wait_ge(g_stats, t + 1)
                    stand_alone(pool)
                    nc.gpsimd.tensor_scalar(ve2[:, 0:1], mv2[:, 0, 1:2], EPS, 1.0, ALU.add, ALU.mult).then_inc(g_scale, 1)
                    pool.wait_ge(g_scale, t * 3 + 1)
                    nc.gpsimd.tensor_tensor(rs2[:, 0:1], ve2[:, 0:1], mhalf[:, 0:1], ALU.pow).then_inc(g_scale, 1)
                    pool.wait_ge(g_scale, t * 3 + 2)
                    stand_alone(pool)
                    nc.gpsimd.tensor_scalar(nb2[:, 0:1], rs2[:, 0:1], mv2[:, 0, 0:1], -1.0, ALU.mult, ALU.mult).then_inc(g_scale, 1)

        @block.scalar
        def _(act):
            for c in range(NKC):
                for h in range(2):
                    n = 2 * c + h
                    act.wait_ge(kproj, n + 1)
                    if c >= 2:
                        act.wait_ge(kt_stored[c % 2], PARTS * DMA * (c // 2))
                    nc.scalar.activation(kth[:, c % 2, h, :], psA[:, 512 * h:512 * h + KC], ACT.Copy).then_inc(kth_ready, 1)
            act.wait_ge(const1_in, NCONST * DMA)
            act.wait_ge(zeroed, 4)
            for p in range(2):
                nc.scalar.activation(kst[MROW:P, p, :, :].rearrange("r s c -> r (s c)"), sel[MROW:P, :],
                                     ACT.Copy).then_inc(kst_ready, 1)

            def step(l, a, m, c, d, f, g):
                def exps(j):
                    if not c.exists:
                        return
                    s0, n = GROUPS[j]
                    e = (6 * c.par + j) % 2
                    act.wait_ge(s_done, c.at(6, j + 1))
                    again = j >= 2 or (c - 1).exists
                    if again:
                        act.wait_ge(pl_ready, c.at(6, j - 1))
                    nc.scalar.activation(E[:, e, 0:n, :], psS[e][:, 0:n * S].rearrange("p (n q) -> p n q", n=n),
                                         ACT.Exp, scale=SCALE).then_inc(e_ready, 1)
                    if again:
                        act.wait_ge(pv_done, c.at(6, j - 1))
                    nc.scalar.activation(ph[:, e, 0:n, :], psS[e][:, 0:n * S].rearrange("p (n q) -> p n q", n=n),
                                         ACT.Exp, scale=SCALE).then_inc(ph_ready, 1)

                exps(0)
                exps(1)
                if a.exists:
                    act.wait_ge(xT_done, a.at(1, 1))
                    nc.scalar.activation(xnT[:, :, :], M1[:, :].rearrange("p (k q) -> p k q", k=2), ACT.Copy).then_inc(xnT_ready, 1)
                exps(2)
                if d.exists:
                    act.wait_ge(oT_done, d.at(1, 1))
                    nc.scalar.activation(onT[:, :, :], M0[:, :].rearrange("p (k q) -> p k q", k=2), ACT.Copy).then_inc(onT_ready, 1)
                if f.exists:
                    act.wait_ge(scale2, f.at(4, 4))
                    for j in range(2):
                        last = nc.scalar.activation(yn[:, j, :], X[:, bass.ds(f.index() * 2 + j, 1), :].rearrange("p a c -> p (a c)"),
                                                    ACT.Identity, scale=rs2[:, j:j + 1], bias=nb2[:, j:j + 1])
                    last.then_inc(yn_ready, 1)
                if a.exists:
                    act.wait_ge(q_done, a.at(1, 1))
                    if (a - 2).exists:
                        act.wait_ge(qst_in[a.par], (a - 2).at2(2 * DMA))
                    nc.scalar.activation(qh[:, a.par, :, :], M1[:, :].rearrange("p (k q) -> p k q", k=2), ACT.Copy).then_inc(qh_ready, 1)
                exps(3)
                if f.exists:
                    act.wait_ge(yT_done, f.at(1, 1))
                    nc.scalar.activation(ynT[:, :, :], M1[:, :].rearrange("p (k q) -> p k q", k=2), ACT.Copy).then_inc(ynT_ready, 1)
                exps(4)
                if m.exists:
                    act.wait_ge(mT_done, m.at(1, 1))
                    if (m - 1).exists:
                        act.wait_ge(m_in[c.par], (m - 1).at2(DMA))
                    nc.scalar.activation(mh[:, :], psA[0:H, 0:S], ACT.Copy).then_inc(mh_ready, 1)
                exps(5)
                if f.exists:
                    act.wait_ge(h_done, f.at(1, 1))
                    nc.scalar.activation(hr[:, :, :], M1[:, 0:2 * (F + NE)].rearrange("p (j f) -> p j f", j=2)[:, :, 0:F],
                                         ACT.Relu).then_inc(hr_ready, 1)
                    act.wait_ge(hT_done, f.at(1, 1))
                    nc.scalar.activation(hT[:, :], M0[:, 0:S], ACT.Square).then_inc(hT_ready, 1)
                if l.exists:
                    act.wait_ge(scale1, l.at(4, 4))
                    if (l - 2).exists:
                        act.wait_ge(xT_done, (l - 2).at(1, 1))
                    for j in range(2):
                        last = nc.scalar.activation(xn[:, l.par, j, :], X[:, bass.ds(l.index() * 2 + j, 1), :].rearrange("p a c -> p (a c)"),
                                                    ACT.Identity, scale=rs1[:, j:j + 1], bias=nb1[:, j:j + 1])
                    last.then_inc(xn_ready, 1)

            schedule(act, step)
            act.wait_ge(top_step, 6)
            nc.scalar.activation(top[:, 3, :], top[:, 2, :], ACT.Exp).then_inc(gap_exp, 1)
            act.wait_ge(flag_ready, 1)
            with act.If(act.value_load(flag[0:1, 0:1]) != 0):
                act.sem_inc(g_hT, 1)
                with act.Fori(0, NT) as t:
                    act.wait_ge(g_scale, t * 3 + 3)
                    nc.scalar.activation(yn[:, 0, :], X[:, bass.ds(t, 1), :].rearrange("p a c -> p (a c)"),
                                         ACT.Identity, scale=rs2[:, 0:1], bias=nb2[:, 0:1]).then_inc(g_yn, 1)
                    act.wait_ge(g_yT, t + 1)
                    nc.scalar.activation(ynT[:, :, 0:P], M0[:, 0:2 * P].rearrange("p (k q) -> p k q", k=2), ACT.Copy).then_inc(g_ynT, 1)
                    for e in range(NE):
                        act.wait_ge(g_h, t * NE + (e + 1))
                        nc.scalar.activation(hr[:, 0, :], M1[:, 0:P], ACT.Relu).then_inc(g_relu, 1)
                        act.wait_ge(g_relu, t * NE + (e + 1))
                        nc.scalar.activation(hT[:, 0:P], hr[:, 0, :], ACT.Square).then_inc(g_hT, 1)

        @block.vector
        def _(dve):
            for c in range(NKC):
                for h in range(2):
                    n = 2 * c + h
                    dve.wait_ge(kth_ready, n + 1)
                    if c >= 2:
                        dve.wait_ge(kt_stored[c % 2], PARTS * DMA * (c // 2))
                    nc.vector.tensor_tensor(ktl[:, c % 2, h, :], psA[:, 512 * h:512 * h + KC],
                                            kth[:, c % 2, h, :].bitcast(FP32), ALU.subtract).then_inc(ktl_ready, 1)

            def step(l, a, m, c, d, f, g):
                def low_part(j):
                    if not c.exists:
                        return
                    s0, n = GROUPS[j]
                    e = (6 * c.par + j) % 2
                    dve.wait_ge(ph_ready, c.at(6, j + 1))
                    if j >= 2 or (c - 1).exists:
                        dve.wait_ge(pv_done, c.at(6, j - 1))
                    nc.vector.tensor_tensor(pl[:, e, 0:n, :], E[:, e, 0:n, :], ph[:, e, 0:n, :], ALU.subtract).then_inc(pl_ready, 1)

                def maximum(j):
                    if not m.exists:
                        return
                    t, h = j // 2, j % 2
                    dve.wait_ge(sa_done, m.at(4, j + 1))
                    if j == 0 and (m - 1).exists:
                        dve.wait_ge(mT_done, (m - 1).at(1, 1))
                    src = psA[:, :].rearrange("p (g c) -> p g c", g=2)[:, :, 0:HG].rearrange("p g (h k) -> p g h k", k=NK)
                    nc.vector.tensor_reduce(nm[:, t, 8 * h:8 * h + 8].rearrange("p (g h) -> p g h", g=2), src, AX.X, ALU.max,
                                            negate=True).then_inc(max_ready, 1)

                def statistics(bt, st, mv, own, stats, used):
                    if (bt - 1).exists:
                        dve.wait_ge(used, (bt - 1).at(4, 4))
                    stand_alone(dve)
                    for j in range(2):
                        nc.vector.bn_stats(st[:, j, :], X[:, bass.ds(bt.index() * 2 + j, 1), :].rearrange("p a c -> p (a c)")).then_inc(own, 1)
                    dve.wait_ge(own, bt.at(2, 2))
                    stand_alone(dve)
                    for j in range(2):
                        nc.vector.bn_aggr(mv[:, j, :], st[:, j, :]).then_inc(stats, 1)

                if d.exists:
                    o = [psO[t][:, 0:H * OC].rearrange("p (h c) -> p h c", c=OC) for t in range(2)]
                    dve.wait_ge(pv_done, d.at(6, 6))
                    for t in range(2):
                        nc.vector.reciprocal(rden[:, t, :].unsqueeze(2), o[t][:, :, HD:OC]).then_inc(den_ready, 1)
                    for t in range(2):
                        dve.wait_ge(den_ready, d.at(2, t + 1))
                        if t == 0 and (d - 1).exists:
                            dve.wait_ge(oT_done, (d - 1).at(1, 1))
                        nc.vector.tensor_tensor(on[:, t, :].rearrange("p (h c) -> p h c", c=HD), o[t][:, :, 0:HD],
                                                rden[:, t, :].unsqueeze(2).to_broadcast([P, H, HD]), ALU.mult).then_inc(on_ready, 1)
                if g.exists:
                    dve.wait_ge(ffn_done, g.at(1, 1))
                    if (g - 2).exists:
                        dve.wait_ge(out_stored[g.par], (g - 2).at2(DMA))
                    nc.vector.tensor_tensor(ost[:, g.par, :, :], M1[:, :].rearrange("p (j c) -> p j c", j=2),
                                            X[:, bass.ds(g.index() * 2, 2), :], ALU.add).then_inc(out_ready, 1)
                low_part(0)
                maximum(0)
                if m.exists:
                    dve.wait_ge(v_done, m.at(1, 1))
                    if (m - 1).exists:
                        dve.wait_ge(v_ready, (m - 1).at(4, 4))
                    nc.vector.tensor_tensor(vf[:, :, :], M0[:, 0:NBLK * HD].rearrange("p (n c) -> p n c", c=HD),
                                            mask[:, :].unsqueeze(2).to_broadcast([P, NBLK, HD]), ALU.mult).then_inc(v_masked, 1)
                low_part(1)
                maximum(1)
                low_part(2)
                maximum(2)
                if l.exists:
                    dve.wait_ge(x_in[l.par], l.at2(DMA))
                    statistics(l, st1, mv1, ln1_step, stats1, scale1)
                if a.exists:
                    dve.wait_ge(qh_ready, a.at(1, 1))
                    if (a - 2).exists:
                        dve.wait_ge(qst_in[a.par], (a - 2).at2(2 * DMA))
                    nc.vector.tensor_tensor(ql[:, a.par, :, :], M1[:, :].rearrange("p (k q) -> p k q", k=2),
                                            qh[:, a.par, :, :].bitcast(FP32), ALU.subtract).then_inc(ql_ready, 1)
                maximum(3)
                low_part(3)
                low_part(4)
                if d.exists:
                    dve.wait_ge(attn_done, d.at(1, 1))
                    xt = X[:, bass.ds(d.index() * 2, 2), :]
                    nc.vector.tensor_tensor(xt, M0[:, :].rearrange("p (j c) -> p j c", j=2), xt, ALU.add).then_inc(y_ready, 1)
                low_part(5)
                if f.exists:
                    dve.wait_ge(hr_ready, f.at(1, 1))
                    nc.vector.tensor_copy(logits[:, bass.ds(f.index() * 2, 2), :],
                                          M1[:, 0:2 * (F + NE)].rearrange("p (j f) -> p j f", j=2)[:, :, F:F + NE]).then_inc(logits_ready, 1)
                if d.exists:
                    dve.wait_ge(y_ready, d.at(1, 1))
                    statistics(d, st2, mv2, ln2_step, stats2, scale2)

            schedule(dve, step)
            k = [0]

            def link(ins):
                k[0] += 1
                ins.then_inc(top_step, 1)
                dve.wait_ge(top_step, k[0])

            dve.wait_ge(logits_ready, NB)
            first, second, gap, e_gap, many = (top[:, n, :] for n in range(5))
            wide = lambda t: t.unsqueeze(2).to_broadcast([P, NT, NE])
            link(nc.vector.tensor_reduce(first, logits[:, :, :], AX.X, ALU.max))
            link(nc.vector.tensor_tensor(prob[:, :, :], logits[:, :, :], wide(first), ALU.is_ge))
            link(nc.vector.tensor_reduce(many, prob[:, :, :], AX.X, ALU.add))
            link(nc.vector.scalar_tensor_tensor(l2[:, :, :], prob[:, :, :], -BIG, logits[:, :, :], ALU.mult, ALU.add))
            link(nc.vector.tensor_reduce(second, l2[:, :, :], AX.X, ALU.max))
            link(nc.vector.tensor_tensor(gap, second, first, ALU.subtract))
            dve.wait_ge(gap_exp, 1)
            link(nc.vector.tensor_scalar(second, e_gap, 1.0, None, ALU.add))
            link(nc.vector.reciprocal(first, second))
            link(nc.vector.tensor_scalar(gap, first, 1.0, None, ALU.is_ge))
            link(nc.vector.scalar_tensor_tensor(first, many, 1.0, gap, ALU.is_equal, ALU.mult))
            link(nc.vector.tensor_tensor(prob[:, :, :], prob[:, :, :], wide(first), ALU.mult))
            link(nc.vector.tensor_reduce(any1[:, :], prob[:, :, :].rearrange("p n e -> p (n e)"), AX.X, ALU.max))
            dve.wait_ge(any_done, 1)
            nc.vector.tensor_copy(flag[0:1, 0:1], M0[0:1, 0:1]).then_inc(flag_ready, 1)
            dve.wait_ge(flag_ready, 1)
            with dve.If(dve.value_load(flag[0:1, 0:1]) != 0):
                dve.sem_inc(g_added, 1)
                with dve.Fori(0, NT) as t:
                    dve.wait_ge(g_added, t * NE + 1)
                    stand_alone(dve)
                    nc.vector.bn_stats(st2[:, 0, :], X[:, bass.ds(t, 1), :].rearrange("p a c -> p (a c)")).then_inc(g_step, 1)
                    dve.wait_ge(g_step, t + 1)
                    stand_alone(dve)
                    nc.vector.bn_aggr(mv2[:, 0, :], st2[:, 0, :]).then_inc(g_stats, 1)
                    dve.wait_ge(g_out_in, t * DMA + DMA)
                    for e in range(NE):
                        dve.wait_ge(g_y, t * NE + (e + 1))
                        dve.wait_ge(g_added, t * NE + (e + 1))
                        nc.vector.scalar_tensor_tensor(gout[:, :], psS[0][:, 0:D],
                                                       prob[:, bass.ds(t, 1), e:e + 1].rearrange("p n e -> p (n e)"),
                                                       gout[:, :], ALU.mult, ALU.add).then_inc(g_added, 1)

        @block.tensor
        def _(pe):
            pe.wait_ge(consts_in, 2 * DMA)
            for c in range(NKC):
                for h in range(2):
                    if c >= 1:
                        pe.wait_ge(ktl_ready, 2 * (c - 1) + h + 1)
                    nc.tensor.matmul(psA[:, 512 * h:512 * h + KC], wk[:, h * P:(h + 1) * P],
                                     z[:, KB * c:KB * (c + 1), :], start=True, stop=True).then_inc(kproj, 1)
            pe.wait_ge(const1_in, NCONST * DMA)
            pe.wait_ge(ktl_ready, 2 * NKC)

            def step(l, a, m, c, d, f, g):
                def scores(j):
                    if not c.exists:
                        return
                    s0, n = GROUPS[j]
                    e = (6 * c.par + j) % 2
                    if j == 0:
                        pe.wait_ge(kst_in[c.par], c.at2(4 * DMA))
                        pe.wait_ge(qst_in[c.par], c.at2(2 * DMA))
                        pe.wait_ge(m_in[c.par], c.at2(DMA))
                    if j >= 2 or (c - 1).exists:
                        pe.wait_ge(ph_ready, c.at(6, j - 1))
                    for u in range(n):
                        last = nc.tensor.matmul(psS[e][:, u * S:(u + 1) * S], kst[:, c.par, s0 + u, :],
                                                qst[:, c.par, s0 + u, :], start=True, stop=True)
                    last.then_inc(s_done, 1)

                def values(j):
                    if not c.exists:
                        return
                    s0, n = GROUPS[j]
                    e = (6 * c.par + j) % 2
                    if j == 0:
                        pe.wait_ge(v_ready, c.at(4, 4))
                        if d.exists:
                            pe.wait_ge(on_ready, d.at(2, 2))
                    pe.wait_ge(pl_ready, c.at(6, j + 1))
                    for t in range(2):
                        for u in range(n):
                            s = s0 + u
                            nh, h0, blk = NHS[s], FIRST[s], VBLK[s]
                            o = psO[t][:, h0 * OC:(h0 + nh) * OC]
                            q = slice(t * P, (t + 1) * P)
                            for k, (p_, v_) in enumerate(((ph, v1), (ph, v2), (ph, v3), (pl, v1), (pl, v2))):
                                last = nc.tensor.matmul(o, p_[:, e, u, q],
                                                        v_[:, c.par, blk:blk + nh, :].rearrange("p n c -> p (n c)"),
                                                        start=(s == 0 and k == 0), stop=(s == NSL - 1 and k == 4),
                                                        skip_group_check=True)
                    last.then_inc(pv_done, 1)

                def maxima_scores(j):
                    if not m.exists:
                        return
                    t, h = j // 2, j % 2
                    if j == 0:
                        pe.wait_ge(kbd_ready, m.at(2, 2))
                        pe.wait_ge(qh_ready, m.at(1, 1))
                        if (m - 1).exists:
                            pe.wait_ge(mh_ready, (m - 1).at(1, 1))
                    else:
                        pe.wait_ge(max_ready, m.at(4, j))
                    for u in range(2):
                        last = nc.tensor.matmul(psA[:, 512 * u:512 * u + HG], qh[:, m.par, h, t * P:(t + 1) * P],
                                                kbd[:, m.par, h, u * HG:(u + 1) * HG], start=True, stop=True)
                    last.then_inc(sa_done, 1)

                def transposes(dst, src, done):
                    for k in range(2):
                        for t in range(2):
                            last = nc.tensor.transpose(dst[:, k * S + t * P:k * S + (t + 1) * P],
                                                       src[:, t, k * P:(k + 1) * P], ident[:, :])
                    last.then_inc(done, 1)

                def project(dst, src, w, done):
                    n = w.shape[-1]
                    for t in range(2):
                        for k in range(2):
                            last = nc.tensor.matmul(dst[:, t * n:(t + 1) * n], src[:, k, t * P:(t + 1) * P], w[:, k, :],
                                                    start=(k == 0), stop=(k == 1))
                    last.then_inc(done, 1)

                scores(0)
                if g.exists:
                    pe.wait_ge(logits_ready, g.at(1, 1))
                    pe.wait_ge(hT_ready, g.at(1, 1))
                    for t in range(2):
                        last = nc.tensor.matmul(M1[:, t * D:(t + 1) * D], hT[:, t * P:(t + 1) * P], ws2[:, :],
                                                start=True, stop=True)
                    last.then_inc(ffn_done, 1)
                maxima_scores(0)
                if m.exists:
                    if g.exists:
                        pe.wait_ge(hT_ready, g.at(1, 1))
                    elif f.exists:
                        pe.wait_ge(y_ready, f.at(1, 1))
                    elif (m - 1).exists:
                        pe.wait_ge(v_masked, (m - 1).at(1, 1))
                    n_a = 11 * HD
                    pe.wait_ge(zc_in[m.par], m.at2(DMA))
                    nc.tensor.matmul(M0[:, 0:n_a], zc[:, m.par, 0:P], wv[:, 0:n_a], start=True, stop=True)
                    nc.tensor.matmul(M0[:, n_a:NBLK * HD], zc[:, m.par, CUT:CUT + P], wv[:, n_a:NBLK * HD],
                                     start=True, stop=True).then_inc(v_done, 1)
                scores(1)
                values(0)
                if a.exists:
                    if g.exists:
                        pe.wait_ge(out_ready, g.at(1, 1))
                    elif (a - 1).exists:
                        pe.wait_ge(ql_ready, (a - 1).at(1, 1))
                    pe.wait_ge(xn_ready, a.at(1, 1))
                    transposes(M1, xn[:, a.par, :, :], xT_done)
                maxima_scores(1)
                if d.exists:
                    if m.exists:
                        pe.wait_ge(v_masked, m.at(1, 1))
                    else:
                        pe.wait_ge(hT_ready, g.at(1, 1))
                    pe.wait_ge(on_ready, d.at(2, 2))
                    transposes(M0, on[:, :, :], oT_done)
                scores(2)
                values(1)
                maxima_scores(2)
                if a.exists:
                    pe.wait_ge(xnT_ready, a.at(1, 1))
                    for h in range(2):
                        for k in range(2):
                            last = nc.tensor.matmul(M1[:, h * S:(h + 1) * S], wq[:, k, h * P:(h + 1) * P], xnT[:, k, :],
                                                    start=(k == 0), stop=(k == 1))
                    last.then_inc(q_done, 1)
                scores(3)
                values(2)
                maxima_scores(3)
                if f.exists:
                    if a.exists:
                        pe.wait_ge(ql_ready, a.at(1, 1))
                    elif g.exists:
                        pe.wait_ge(out_ready, g.at(1, 1))
                    pe.wait_ge(yn_ready, f.at(1, 1))
                    transposes(M1, yn[:, :, :], yT_done)
                scores(4)
                if d.exists:
                    pe.wait_ge(onT_ready, d.at(1, 1))
                    project(M0, onT, wo, attn_done)
                if m.exists:
                    pe.wait_ge(max_ready, m.at(4, 4))
                    for t in range(2):
                        last = nc.tensor.transpose(psA[0:H, t * P:(t + 1) * P], nm[:, t, :], ident[:, :])
                    last.then_inc(mT_done, 1)
                values(3)
                scores(5)
                if f.exists:
                    pe.wait_ge(ynT_ready, f.at(1, 1))
                    project(M1, ynT, w1r, h_done)
                values(4)
                if f.exists:
                    if d.exists:
                        pe.wait_ge(y_ready, d.at(1, 1))
                    else:
                        pe.wait_ge(hT_ready, g.at(1, 1))
                    pe.wait_ge(hr_ready, f.at(1, 1))
                    for t in range(2):
                        last = nc.tensor.transpose(M0[:, t * P:(t + 1) * P], hr[:, t, :], ident[:, :])
                    last.then_inc(hT_done, 1)
                values(5)

            schedule(pe, step)
            pe.wait_ge(top_step, 12)
            pe.wait_ge(hT_ready, NB)
            nc.tensor.matmul(M0[0:1, 0:1], any1[:, :], ones[:, :], start=True, stop=True).then_inc(any_done, 1)
            pe.wait_ge(flag_ready, 1)
            with pe.If(pe.value_load(flag[0:1, 0:1]) != 0):
                pe.wait_ge(experts_in, 2 * DMA)
                with pe.Fori(0, NT) as t:
                    pe.wait_ge(g_yn, t + 1)
                    for k in range(2):
                        last = nc.tensor.transpose(M0[:, k * P:(k + 1) * P], yn[:, 0, k * P:(k + 1) * P], ident[:, :])
                    last.then_inc(g_yT, 1)
                    pe.wait_ge(g_ynT, t + 1)
                    for e in range(NE):
                        pe.wait_ge(g_hT, t * NE + (e + 1))
                        for k in range(2):
                            last = nc.tensor.matmul(M1[:, 0:P], w1[:, k, e, :], ynT[:, k, 0:P], start=(k == 0), stop=(k == 1))
                        last.then_inc(g_h, 1)
                        pe.wait_ge(g_hT, t * NE + (e + 2))
                        pe.wait_ge(g_added, t * NE + (e + 1))
                        nc.tensor.matmul(psS[0][:, 0:D], hT[:, 0:P], w2[:, e, :], start=True, stop=True).then_inc(g_y, 1)


def kernel(x, ctx_512, L0_xattn_Wq, L0_xattn_Wkv, L0_xattn_Wo, L0_ffn_Ws1, L0_ffn_Ws2, L0_ffn_W1, L0_ffn_W2,
           L0_ffn_Wr):
    import numpy as np
    import concourse.bacc as bacc
    from concourse.bass_utils import run_bass_kernel_spmd

    f32 = np.float32
    cols = lambda w: w.reshape(2, P, -1).transpose(1, 0, 2)
    zt = ctx_512.transpose(2, 0, 1)
    wvt = L0_xattn_Wkv[D:].T.reshape(LAT, H, HD)
    order = [h for i in range(6) for h in (3 * i, 3 * i + 1) if h < H] + [h for i in range(5) for h in (3 * i + 1, 3 * i + 2)]
    row = np.arange(P)
    mask = np.zeros((P, NBLK), f32)
    sel = np.zeros((2, H, NSL, P), f32)
    for s in range(NSL):
        spans = ((0, NK), (NK, P)) if s % 2 == 0 else ((0, REST), (REST, REST + NK))
        for n in range(NHS[s]):
            own = (row >= spans[n][0]) & (row < spans[n][1])
            mask[:, VBLK[s] + n] = own
            sel[0, FIRST[s] + n, s, :] = own
    arrays = {
        "x": x.reshape(NB * S, D),
        "z": zt,
        "zz": np.concatenate([zt, zt, zt[:, :, :REST]], axis=2),
        "wq": cols(L0_xattn_Wq.T),
        "wk": L0_xattn_Wkv[:D].T,
        "wv": wvt[:, order, :].reshape(LAT, NBLK * HD),
        "wo": cols(L0_xattn_Wo.T),
        "w1r": cols(np.concatenate([L0_ffn_Ws1, L0_ffn_Wr], axis=1)),
        "ws2": L0_ffn_Ws2,
        "w1": L0_ffn_W1.reshape(NE, 2, P, F).transpose(2, 1, 0, 3),
        "w2": L0_ffn_W2.transpose(1, 0, 2),
        "ident": np.eye(P, dtype=f32),
        "mask": mask,
        "headmask": (row[:, None] // HD == np.arange(8)).astype(f32),
        "sel": sel.reshape(32, NSL * P),
    }
    arrays = {n: np.ascontiguousarray(a) for n, a in arrays.items()}
    nc = bacc.Bacc("TRN2", target_bir_lowering=False, num_devices=1)
    args = [nc.dram_tensor(f"in_{n}", a.shape, FP32, kind="ExternalInput").ap() for n, a in arrays.items()]
    out = nc.dram_tensor("out", (NB * S, D), FP32, kind="ExternalOutput").ap()
    build(nc, *args, out)
    r = run_bass_kernel_spmd(nc, [{f"in_{n}": a for n, a in arrays.items()}], core_ids=[0])
    return r.results[0]["out"].reshape(NB, S, D)
```

```python
import concourse.bass as bass
from concourse import mybir
from concourse.alu_op_type import AluOpType as ALU
from contextlib import ExitStack

FP32 = mybir.dt.float32
FP32R = mybir.dt.float32r
BF16 = mybir.dt.bfloat16
FP16 = mybir.dt.float16
I32 = mybir.dt.int32
ACT = mybir.ActivationFunctionType
AX = mybir.AxisListType

P = 128
NB, S, D = 32, 256, 256
NT = NB * S // P
LAT, NK = 128, 77
H, HD = 16, 16
F, NE = 128, 8
EPS = 1e-5
SCALE = HD ** -0.5
BIG = 3.0e38

PARTS = 3
HR = PARTS * HD
MROW = 2 * HR
CUT = P - NK
REST = NK - CUT
ZW = 2 * NK + REST
NSL = 11
FIRST = [3 * (s // 2) + s % 2 for s in range(NSL)]
NHS = [min(2, H - f) for f in FIRST]
VBLK = [2 * (s // 2) if s % 2 == 0 else 11 + 2 * (s // 2) for s in range(NSL)]
NBLK = 21
GROUPS = [(2 * j, min(2, NSL - 2 * j)) for j in range(6)]
NCONST = 7
OC = HD + 1
HG = 4 * NK
KB = 4
NKC = NB // KB
KC = KB * NK
KPARTS = ((0, 1), (1, 4), (4, NKC))
STORES = [(k, n) for k in range(1, len(KPARTS)) for n in range(PARTS)]
DMA = 16


class Batch:

    def __init__(self, i, k):
        self.i, self.k = i, k

    def __add__(self, d):
        return Batch(self.i, self.k + d)

    def __sub__(self, d):
        return Batch(self.i, self.k - d)

    @property
    def exists(self):
        return not isinstance(self.i, int) or 0 <= self.k < NB

    @property
    def par(self):
        return self.k % 2

    def at(self, per, j):
        return self.i * (UNROLL * per) + (self.k * per + j)

    def at2(self, per):
        return self.i * (UNROLL // 2 * per) + (self.k // 2 + 1) * per

    def index(self):
        return self.i * UNROLL + self.k


LOOP_FROM, LOOP_TO = 8, 28
UNROLL = 4


def key_part(b):
    return b.k + 1 if isinstance(b.i, int) and b.k + 1 < len(KPARTS) else None


def schedule(eng, step, between=()):
    def call(s):
        step(*(s + n for n in (3, 2, 1, 0, -1, -2, -3)))
    for s in range(-3, LOOP_FROM):
        call(Batch(0, s))
    with eng.Fori(LOOP_FROM // UNROLL, LOOP_TO // UNROLL) as i:
        for k in range(UNROLL):
            call(Batch(i, k))
    for s in range(LOOP_TO, NB + 3):
        if s in between:
            between[s]()
        call(Batch(0, s))


def build(nc, x_d, z_d, zz_d, wq_d, wk_d, wv_d, wo_d, w1r_d, ws2_d, w1_d, w2_d, ident_d, mask_d, headmask_d, sel_d, out_d):
    kt_d = nc.dram_tensor("kt_scratch", (2 * P, PARTS, NB * NK), FP32, kind="Internal").ap()
    qt_d = nc.dram_tensor("qt_scratch", (2, (H + 2) * HD, PARTS, S), FP32, kind="Internal").ap()
    ctx = ExitStack()
    with ctx:
        def sb(name, shape, dt=FP32):
            return ctx.enter_context(nc.sbuf_tensor(name, shape, dt))

        def sem(name):
            return ctx.enter_context(nc.semaphore(name))

        def sem2(name):
            return [sem(f"{name}{p}") for p in range(2)]

        X = sb("X", [P, NT, D])
        zw = sb("zw", [P, 2 * NE * F + NE * D])
        z = zw[:, 0:NB * NK].rearrange("p (b k) -> p b k", k=NK)
        sel = zw[:, NB * NK:NB * NK + NSL * P]
        w1 = zw[:, 0:2 * NE * F].rearrange("p (k e f) -> p k e f", k=2, e=NE)
        w2 = zw[:, 2 * NE * F:].rearrange("p (e d) -> p e d", e=NE)
        zc = sb("zc", [P, 2, ZW])
        wq = sb("wq", [P, 2, D])
        wk = sb("wk", [P, D])
        wv = sb("wv", [P, NBLK * HD])
        wo = sb("wo", [P, 2, D])
        w1r = sb("w1r", [P, 2, F + NE])
        ws2 = sb("ws2", [P, D])
        ident = sb("ident", [P, P])
        mask = sb("mask", [P, NBLK])
        k_out = X[:, NT - 40:NT, :].rearrange("p n c -> p (n c)")[:, 0:4 * NB * NK].bitcast(FP32R)
        kth, ktl = (k_out[:, n * 2 * NB * NK:(n + 1) * 2 * NB * NK].rearrange("p (h c) -> p h c", h=2) for n in range(2))
        kT = sb("kT", [P, 2, 2, NK])
        headmask = sb("headmask", [P, 8])
        kbd = sb("kbd", [P, 2, 2, 8 * NK], FP32R)
        kst = sb("kst", [P, 2, NSL, P], FP32R)
        qst = sb("qst", [P, 2, NSL, S], FP32R)
        st1 = sb("st1", [P, 2, 6])
        mv1 = sb("mv1", [P, 2, 2])
        ve1 = sb("ve1", [P, 2])
        rs1 = sb("rs1", [P, 2])
        nb1 = sb("nb1", [P, 2])
        st2 = sb("st2", [P, 2, 6])
        mv2 = sb("mv2", [P, 2, 2])
        ve2 = sb("ve2", [P, 2])
        rs2 = sb("rs2", [P, 2])
        nb2 = sb("nb2", [P, 2])
        mhalf = sb("mhalf", [P, 2])
        xn = sb("xn", [P, 2, D])
        xnT = sb("xnT", [P, 2, S])
        qh = sb("qh", [P, 2, 2, S], FP32R)
        ql = sb("ql", [P, 2, 2, S], FP32R)
        nm = sb("nm", [P, 2, H])
        mh = sb("mh", [H, S], FP32R)
        vf = sb("vf", [P, NBLK, HD])
        vr = sb("vr", [P, NBLK, HD])
        v1 = sb("v1", [P, 2, NBLK, OC], BF16)
        v2 = sb("v2", [P, 2, NBLK, OC], BF16)
        v3 = sb("v3", [P, 2, NBLK, OC], BF16)
        E = sb("E", [P, 2, 2, S])
        ph = sb("ph", [P, 2, 2, S], FP16)
        pl = sb("pl", [P, 2, 2, S], FP16)
        rden = sb("rden", [P, 2, H])
        on = sb("on", [P, 2, D])
        onT = sb("onT", [P, 2, S])
        yn = sb("yn", [P, 2, D])
        ynT = sb("ynT", [P, 2, S])
        hr = sb("hr", [P, 2, F])
        hT = sb("hT", [P, S])
        ost = sb("ost", [P, 2, 2, D])
        logits = sb("logits", [P, NT, NE])
        prob = sb("prob", [P, NT, NE])
        top = sb("top", [P, 5, NT])
        ones = sb("ones", [P, 1])
        any1 = sb("any1", [P, 1])
        flag = sb("flag", [1, 1], I32)
        l2 = sb("l2", [P, NT, NE])
        gout = sb("gout", [P, D])

        def pb(name, cols):
            return ctx.enter_context(nc.psum_tensor(name, [P, cols], FP32))

        psS = [pb(f"psS{j}", 512) for j in range(2)]
        psO = [pb(f"psO{j}", 512) for j in range(2)]
        psA = pb("psA", 1024)
        M0, M1 = pb("M0", 512), pb("M1", 512)
        key_bank = psS + psO

        consts_in = sem("consts_in")
        const1_in = sem("const1_in")
        experts_in = sem("experts_in")
        x_in = sem2("x_in")
        zc_in = sem2("zc_in")
        kT_in = sem2("kT_in")
        qt_stored = sem2("qt_stored")
        pad_stored = sem("pad_stored")
        kbd_ready = sem("kbd_ready")
        kst_in = sem2("kst_in")
        qst_in = sem2("qst_in")
        m_in = sem2("m_in")
        out_stored = sem2("out_stored")
        kt_stored = sem("kt_stored")
        z_rest_in, query_consts_in = sem("z_rest_in"), sem("query_consts_in")
        zeroed, qst_zeroed = sem("zeroed"), sem("qst_zeroed")
        kst_ready = sem("kst_ready")
        kproj, kth_ready, ktl_ready = sem("kproj"), sem("kth_ready"), sem("ktl_ready")
        stats1, scale1, xn_ready = sem("stats1"), sem("scale1"), sem("xn_ready")
        v_done, v_masked, v_ready = sem("v_done"), sem("v_masked"), sem("v_ready")
        pool_step = sem("pool_step")
        ln1_step, ln2_step = sem("ln1_step"), sem("ln2_step")
        xT_done, xnT_ready = sem("xT_done"), sem("xnT_ready")
        q_done, qh_ready, ql_ready = sem("q_done"), sem("qh_ready"), sem("ql_ready")
        sa_done, max_ready = sem("sa_done"), sem("max_ready")
        mT_done, mh_ready = sem("mT_done"), sem("mh_ready")
        s_done, ph_ready, pl_ready = sem("s_done"), sem("ph_ready"), sem("pl_ready")
        pv_done, den_ready, on_ready = sem("pv_done"), sem("den_ready"), sem("on_ready")
        oT_done, onT_ready = sem("oT_done"), sem("onT_ready")
        attn_done, y_ready = sem("attn_done"), sem("y_ready")
        stats2, scale2, yn_ready = sem("stats2"), sem("scale2"), sem("yn_ready")
        yT_done, ynT_ready = sem("yT_done"), sem("ynT_ready")
        h_done, hr_ready, logits_ready = sem("h_done"), sem("hr_ready"), sem("logits_ready")
        hT_done, hT_ready = sem("hT_done"), sem("hT_ready")
        ffn_done, out_ready = sem("ffn_done"), sem("out_ready")
        top_step, gap_exp, any_done, flag_ready = sem("top_step"), sem("gap_exp"), sem("any_done"), sem("flag_ready")
        E_ = mybir.EngineType
        passed = {e: sem(f"passed_{e.name}") for e in (E_.SP, E_.DVE, E_.Pool)}
        g_out_in, g_stored, g_added = sem("g_out_in"), sem("g_stored"), sem("g_added")
        g_step, g_stats, g_scale, g_yn = sem("g_step"), sem("g_stats"), sem("g_scale"), sem("g_yn")
        g_yT, g_ynT, g_h, g_relu = sem("g_yT"), sem("g_ynT"), sem("g_h"), sem("g_relu")
        g_hT, g_y = sem("g_hT"), sem("g_y")

        def stand_alone(eng):
            eng.sem_inc(passed[eng.engine], 1)

        x_t = x_d.rearrange("(n j p) d -> p n j d", p=P, j=2)
        out_t = out_d.rearrange("(n j p) d -> p n j d", p=P, j=2)

        block = ctx.enter_context(nc.Block())

        @block.sync
        def _(sp):
            def load_x0(b):
                sp.dma_start(X[:, 2 * b:2 * b + 2, :], x_t[:, b]).then_inc(x_in[b], DMA)

            z0 = KB * KPARTS[0][1]
            sp.dma_start(wk[:, :], wk_d).then_inc(consts_in, DMA)
            sp.dma_start(z[:, 0:z0, :], z_d[:, 0:z0, :]).then_inc(consts_in, DMA)
            load_x0(0)
            for dst, src in ((ident[:, :], ident_d), (wq[:, :, :], wq_d)):
                sp.dma_start(dst, src).then_inc(query_consts_in, DMA)
            load_x0(1)
            sp.dma_start(z[:, z0:NB, :], z_d[:, z0:NB, :]).then_inc(z_rest_in, DMA)
            for dst, src in ((sel[MROW:P, :], sel_d), (mask[:, :], mask_d), (headmask[:, :], headmask_d),
                             (wv[:, :], wv_d), (wo[:, :, :], wo_d), (w1r[:, :, :], w1r_d), (ws2[:, :], ws2_d)):
                sp.dma_start(dst, src).then_inc(const1_in, DMA)
            for b in range(2):
                sp.dma_start(zc[:, b, :], zz_d[:, b, :]).then_inc(zc_in[b], DMA)

            def store_keys(part, n):
                c0, c1 = KPARTS[part]
                dst = kt_d[:, :, c0 * KC:c1 * KC].rearrange("(h p) n c -> p h n c", p=P)
                src = ktl if n == 2 else kth
                sp.wait_ge(ktl_ready if n == 2 else kth_ready, 2 * c1)
                sp.dma_start(dst[:, :, n, :], src[:, :, c0 * KC:c1 * KC].bitcast(FP32)).then_inc(kt_stored, DMA)

            store_keys(0, 0)
            store_keys(0, 1)
            sp.wait_ge(kt_stored, 2 * DMA)

            kt_rows = kt_d.rearrange("r n (b k) -> (r n) b k", k=NK).rearrange("(i r) b k -> r i b k", r=HR)
            kt_high = kt_d[:, 0, :].rearrange("(h p) (b k) -> p h b k", p=P, k=NK)

            def load_kT(b):
                sp.dma_start(kT[:, b.par, :, :], kt_high[:, :, bass.ds(b.index(), 1), :].rearrange("p h b k -> p h (b k)")
                             ).then_inc(kT_in[b.par], DMA)

            def load_kst(b):
                roles = ((0, 0, 6, 0, 0, NK, 0), (1, 0, 5, HR, NK, P, 0),
                         (1, 1, 5, 0, 0, REST, CUT), (2, 1, 5, HR, REST, REST + NK, 0))
                for head, first, n, r, c0, c1, k0 in roles:
                    src = kt_rows[:, head:head + 3 * (n - 1) + 1:3, bass.ds(b.index(), 1), k0:k0 + c1 - c0]
                    sp.dma_start(kst[r:r + HR, b.par, first:first + 2 * (n - 1) + 1:2, c0:c1].bitcast(FP32),
                                 src.rearrange("r i b k -> r i (b k)")).then_inc(kst_in[b.par], DMA)

            def store_q(b, part, n):
                sp.dma_start(qt_d[b.par, 0:H * HD, n, :].rearrange("(h p) q -> p h q", p=P),
                             part[:, b.par, :, :].bitcast(FP32)).then_inc(qt_stored[b.par], DMA)

            def stack_q(b):
                src = qt_d[b.par].rearrange("r n q -> (r n) q").rearrange("(i r) q -> r i q", r=3 * HR)
                sp.dma_start(qst[0:2 * HR, b.par, 0:NSL:2, :].bitcast(FP32), src[0:2 * HR]).then_inc(qst_in[b.par], DMA)
                sp.dma_start(qst[0:2 * HR, b.par, 1:NSL:2, :].bitcast(FP32), src[HR:3 * HR, 0:5]).then_inc(qst_in[b.par], DMA)

            def step(l, a, m, c, d, f, g):
                if isinstance(m.i, int) and m.k == 0:
                    sp.wait_ge(pad_stored, 2 * DMA)
                    sp.wait_ge(qst_zeroed, 2)
                    sp.wait_ge(kst_ready, 2)
                    sp.wait_ge(kt_stored, PARTS * DMA)
                if isinstance(c.i, int) and 0 <= c.k < len(STORES):
                    sp.wait_ge(kt_stored, (PARTS + c.k + 1) * DMA)
                if m.exists:
                    if (c - 1).exists:
                        sp.wait_ge(s_done, (c - 1).at(6, 6))
                        stand_alone(sp)
                        sp.wait_ge(kst_in[m.par], (m - 2).at2(4 * DMA))
                        stand_alone(sp)
                        sp.wait_ge(m_in[m.par], (m - 2).at2(DMA))
                        stand_alone(sp)
                    load_kst(m)
                    sp.wait_ge(qt_stored[m.par], m.at2(PARTS * DMA))
                    stand_alone(sp)
                    stack_q(m)
                nx = l + 1
                if nx.exists and (nx - 2).exists:
                    sp.wait_ge(x_in[nx.par], (nx - 2).at2(DMA))
                    stand_alone(sp)
                    sp.dma_start(X[:, bass.ds(nx.index() * 2, 2), :],
                                 x_t[:, bass.ds(nx.index(), 1)].rearrange("p n j d -> p (n j) d")
                                 ).then_inc(x_in[nx.par], DMA)
                if l.exists:
                    if (l - 2).exists:
                        sp.wait_ge(kbd_ready, (l - 2).at(2, 2))
                        stand_alone(sp)
                    load_kT(l)
                if isinstance(l.i, int) and l.k == 0:
                    store_keys(0, 2)
                    sp.wait_ge(zeroed, 2)
                    for p in range(2):
                        sp.dma_start(qt_d[p, H * HD:(H + 1) * HD].rearrange("r n q -> (r n) q"),
                                     kst[0:HR, p, 0:S // P, :].rearrange("r s c -> r (s c)").bitcast(FP32)).then_inc(pad_stored, DMA)
                if a.exists and (a - 2).exists:
                    sp.wait_ge(v_done, (a - 2).at(1, 1))
                    stand_alone(sp)
                    sp.dma_start(zc[:, a.par, :], zz_d[:, bass.ds(a.index(), 1), :].rearrange("p b c -> p (b c)")
                                 ).then_inc(zc_in[a.par], DMA)
                if g.exists:
                    sp.wait_ge(out_ready, g.at(1, 1))
                    stand_alone(sp)
                    sp.dma_start(out_t[:, bass.ds(g.index(), 1)].rearrange("p n j d -> p (n j) d"),
                                 ost[:, g.par, :, :]).then_inc(out_stored[g.par], DMA)
                if isinstance(m.i, int) and 0 <= m.k < len(STORES):
                    store_keys(*STORES[m.k])
                if a.exists:
                    sp.wait_ge(qh_ready, a.at(1, 1))
                    stand_alone(sp)
                    store_q(a, qh, 0)
                    store_q(a, qh, 2)
                    sp.wait_ge(ql_ready, a.at(1, 1))
                    stand_alone(sp)
                    store_q(a, ql, 1)
                if m.exists:
                    sp.wait_ge(mh_ready, m.at(1, 1))
                    stand_alone(sp)
                    sp.dma_start(qst[MROW:MROW + H, m.par, :, :].bitcast(FP32),
                                 mh[:, :].bitcast(FP32).unsqueeze(1).to_broadcast([H, NSL, S])).then_inc(m_in[m.par], DMA)

            schedule(sp, step)
            for p in range(2):
                sp.wait_ge(out_stored[p], DMA * NB // 2)
            sp.wait_ge(flag_ready, 1)
            with sp.If(sp.value_load(flag[0:1, 0:1]) != 0):
                sp.dma_start(w1[:, :, :, :], w1_d).then_inc(experts_in, DMA)
                sp.dma_start(w2[:, :, :], w2_d).then_inc(experts_in, DMA)
                out_n = out_d.rearrange("(n p) d -> p n d", p=P)
                sp.sem_inc(g_stored, DMA)
                with sp.Fori(0, NT) as t:
                    sp.wait_ge(g_stored, t * DMA + DMA)
                    stand_alone(sp)
                    sp.dma_start(gout[:, :], out_n[:, bass.ds(t, 1), :].rearrange("p n d -> p (n d)")).then_inc(g_out_in, DMA)
                    sp.wait_ge(g_added, t * NE + (NE + 1))
                    stand_alone(sp)
                    sp.dma_start(out_n[:, bass.ds(t, 1), :].rearrange("p n d -> p (n d)"), gout[:, :]).then_inc(g_stored, DMA)
                sp.wait_ge(g_stored, NT * DMA + DMA)

        @block.gpsimd
        def _(pool):
            nc.gpsimd.memset(mhalf[:, :], -0.5).then_inc(pool_step, 1)
            nc.gpsimd.memset(ones[:, :], 1.0).then_inc(pool_step, 1)
            nc.gpsimd.memset(kst[:, 0].bitcast(FP32), 0.0).then_inc(zeroed, 1)
            nc.gpsimd.memset(kst[:, 1].bitcast(FP32), 0.0).then_inc(zeroed, 1)
            nc.gpsimd.memset(v2[:, :, :, :], 0.0).then_inc(pool_step, 1)
            nc.gpsimd.memset(v3[:, :, :, :], 0.0).then_inc(pool_step, 1)
            pool.wait_ge(pool_step, 4)

            def rsqrt(stats, scale, mv, ve, rs, nb, bt):
                pool.wait_ge(stats, bt.at(2, 2))
                if (bt - 1).exists:
                    pool.wait_ge(xn_ready if scale is scale1 else yn_ready, (bt - 1).at(1, 1))
                stand_alone(pool)
                nc.gpsimd.tensor_scalar(ve[:, :], mv[:, :, 1], EPS, 1.0, ALU.add, ALU.mult).then_inc(scale, 1)
                pool.wait_ge(scale, bt.at(4, 1))
                nc.gpsimd.tensor_tensor(rs[:, :], ve[:, :], mhalf[:, :], ALU.pow).then_inc(scale, 1)
                pool.wait_ge(scale, bt.at(4, 2))
                stand_alone(pool)
                for j in range(2):
                    nc.gpsimd.tensor_scalar(nb[:, j:j + 1], rs[:, j:j + 1], mv[:, j, 0:1], -1.0,
                                            ALU.mult, ALU.mult).then_inc(scale, 1)

            def split_v(b):
                pool.wait_ge(v_masked, b.at(1, 1))
                if (b - 2).exists:
                    pool.wait_ge(pv_done, (b - 2).at(6, 6))
                stand_alone(pool)
                p = b.par
                nc.gpsimd.tensor_copy(v1[:, p, :, 0:HD], vf[:, :, :]).then_inc(v_ready, 1)
                pool.wait_ge(v_ready, b.at(4, 1))
                nc.gpsimd.tensor_tensor(vr[:, :, :], vf[:, :, :], v1[:, p, :, 0:HD], ALU.subtract).then_inc(v_ready, 1)
                pool.wait_ge(v_ready, b.at(4, 2))
                stand_alone(pool)
                nc.gpsimd.tensor_copy(v2[:, p, :, 0:HD], vr[:, :, :]).then_inc(v_ready, 1)
                pool.wait_ge(v_ready, b.at(4, 3))
                nc.gpsimd.tensor_tensor(v3[:, p, :, 0:HD], vr[:, :, :], v2[:, p, :, 0:HD], ALU.subtract).then_inc(v_ready, 1)

            def diagonal_keys(b):
                pool.wait_ge(kT_in[b.par], b.at2(DMA))
                stand_alone(pool)
                if (b - 2).exists:
                    pool.wait_ge(sa_done, (b - 2).at(4, 4))
                    stand_alone(pool)
                for h in range(2):
                    nc.gpsimd.tensor_tensor(kbd[:, b.par, h, :].rearrange("p (h k) -> p h k", k=NK),
                                            kT[:, b.par, h, :].unsqueeze(1).to_broadcast([P, 8, NK]),
                                            headmask[:, :].unsqueeze(2).to_broadcast([P, 8, NK]), ALU.mult).then_inc(kbd_ready, 1)

            def step(l, a, m, c, d, f, g):
                if f.exists:
                    rsqrt(stats2, scale2, mv2, ve2, rs2, nb2, f)
                if l.exists:
                    rsqrt(stats1, scale1, mv1, ve1, rs1, nb1, l)
                    if isinstance(l.i, int) and l.k == 0:
                        pool.wait_ge(const1_in, NCONST * DMA)
                        for p in range(2):
                            nc.gpsimd.tensor_copy(v1[:, p, :, HD:OC], mask[:, :].unsqueeze(2)).then_inc(pool_step, 1)
                        pool.wait_ge(pool_step, 6)
                    diagonal_keys(l)
                if m.exists:
                    split_v(m)

            schedule(pool, step)
            pool.wait_ge(flag_ready, 1)
            with pool.If(pool.value_load(flag[0:1, 0:1]) != 0):
                with pool.Fori(0, NT) as t:
                    pool.wait_ge(g_stats, t + 1)
                    stand_alone(pool)
                    nc.gpsimd.tensor_scalar(ve2[:, 0:1], mv2[:, 0, 1:2], EPS, 1.0, ALU.add, ALU.mult).then_inc(g_scale, 1)
                    pool.wait_ge(g_scale, t * 3 + 1)
                    nc.gpsimd.tensor_tensor(rs2[:, 0:1], ve2[:, 0:1], mhalf[:, 0:1], ALU.pow).then_inc(g_scale, 1)
                    pool.wait_ge(g_scale, t * 3 + 2)
                    stand_alone(pool)
                    nc.gpsimd.tensor_scalar(nb2[:, 0:1], rs2[:, 0:1], mv2[:, 0, 0:1], -1.0, ALU.mult, ALU.mult).then_inc(g_scale, 1)

        @block.scalar
        def _(act):
            def keys(part):
                for c in range(*KPARTS[part]):
                    for h in range(2):
                        n = 2 * c + h
                        act.wait_ge(kproj, n + 1)
                        nc.scalar.activation(kth[:, h, c * KC:(c + 1) * KC], key_bank[n % 4][:, 0:KC], ACT.Copy).then_inc(kth_ready, 1)

            def step(l, a, m, c, d, f, g):
                def exps(j):
                    if not c.exists:
                        return
                    s0, n = GROUPS[j]
                    e = (6 * c.par + j) % 2
                    act.wait_ge(s_done, c.at(6, j + 1))
                    again = j >= 2 or (c - 1).exists
                    if again:
                        act.wait_ge(pl_ready, c.at(6, j - 1))
                    nc.scalar.activation(E[:, e, 0:n, :], psS[e][:, 0:n * S].rearrange("p (n q) -> p n q", n=n),
                                         ACT.Exp, scale=SCALE)
                    if again:
                        act.wait_ge(pv_done, c.at(6, j - 1))
                    nc.scalar.activation(ph[:, e, 0:n, :], psS[e][:, 0:n * S].rearrange("p (n q) -> p n q", n=n),
                                         ACT.Exp, scale=SCALE).then_inc(ph_ready, 1)

                exps(0)
                exps(1)
                if a.exists:
                    act.wait_ge(xT_done, a.at(1, 1))
                    nc.scalar.activation(xnT[:, :, :], M1[:, :].rearrange("p (k q) -> p k q", k=2), ACT.Copy).then_inc(xnT_ready, 1)
                exps(2)
                if f.exists:
                    act.wait_ge(scale2, f.at(4, 4))
                    for j in range(2):
                        last = nc.scalar.activation(yn[:, j, :], X[:, bass.ds(f.index() * 2 + j, 1), :].rearrange("p a c -> p (a c)"),
                                                    ACT.Identity, scale=rs2[:, j:j + 1], bias=nb2[:, j:j + 1])
                    last.then_inc(yn_ready, 1)
                if d.exists:
                    act.wait_ge(oT_done, d.at(1, 1))
                    nc.scalar.activation(onT[:, :, :], M0[:, :].rearrange("p (k q) -> p k q", k=2), ACT.Copy).then_inc(onT_ready, 1)
                if a.exists:
                    act.wait_ge(q_done, a.at(1, 1))
                    if (a - 2).exists:
                        act.wait_ge(qst_in[a.par], (a - 2).at2(2 * DMA))
                    nc.scalar.activation(qh[:, a.par, :, :], M1[:, :].rearrange("p (k q) -> p k q", k=2), ACT.Copy).then_inc(qh_ready, 1)
                if isinstance(a.i, int) and a.k == 0:
                    act.wait_ge(const1_in, NCONST * DMA)
                    act.wait_ge(zeroed, 2)
                    for p in range(2):
                        nc.scalar.activation(kst[MROW:P, p, :, :].rearrange("r s c -> r (s c)"), sel[MROW:P, :],
                                             ACT.Copy).then_inc(kst_ready, 1)
                if key_part(a) is not None:
                    keys(key_part(a))
                exps(3)
                if m.exists:
                    act.wait_ge(mT_done, m.at(1, 1))
                    if (m - 1).exists:
                        act.wait_ge(m_in[c.par], (m - 1).at2(DMA))
                    nc.scalar.activation(mh[:, :], psA[0:H, 0:S], ACT.Copy).then_inc(mh_ready, 1)
                exps(4)
                if l.exists:
                    act.wait_ge(scale1, l.at(4, 4))
                    if a.exists:
                        act.wait_ge(xT_done, a.at(1, 1))
                    for j in range(2):
                        last = nc.scalar.activation(xn[:, j, :], X[:, bass.ds(l.index() * 2 + j, 1), :].rearrange("p a c -> p (a c)"),
                                                    ACT.Identity, scale=rs1[:, j:j + 1], bias=nb1[:, j:j + 1])
                    last.then_inc(xn_ready, 1)
                if f.exists:
                    act.wait_ge(yT_done, f.at(1, 1))
                    nc.scalar.activation(ynT[:, :, :], M1[:, :].rearrange("p (k q) -> p k q", k=2), ACT.Copy).then_inc(ynT_ready, 1)
                exps(5)
                if f.exists:
                    act.wait_ge(h_done, f.at(1, 1))
                    nc.scalar.activation(hr[:, :, :], M1[:, 0:2 * (F + NE)].rearrange("p (j f) -> p j f", j=2)[:, :, 0:F],
                                         ACT.Relu).then_inc(hr_ready, 1)
                    act.wait_ge(hT_done, f.at(1, 1))
                    nc.scalar.activation(hT[:, :], M0[:, 0:S], ACT.Square).then_inc(hT_ready, 1)

            def gap_exponentials():
                act.wait_ge(top_step, 12)
                nc.scalar.activation(top[:, 3, :], top[:, 2, :], ACT.Exp).then_inc(gap_exp, 1)

            schedule(act, step, {NB + 2: gap_exponentials})
            act.wait_ge(flag_ready, 1)
            with act.If(act.value_load(flag[0:1, 0:1]) != 0):
                act.sem_inc(g_hT, 1)
                with act.Fori(0, NT) as t:
                    act.wait_ge(g_scale, t * 3 + 3)
                    nc.scalar.activation(yn[:, 0, :], X[:, bass.ds(t, 1), :].rearrange("p a c -> p (a c)"),
                                         ACT.Identity, scale=rs2[:, 0:1], bias=nb2[:, 0:1]).then_inc(g_yn, 1)
                    act.wait_ge(g_yT, t + 1)
                    nc.scalar.activation(ynT[:, :, 0:P], M0[:, 0:2 * P].rearrange("p (k q) -> p k q", k=2), ACT.Copy).then_inc(g_ynT, 1)
                    for e in range(NE):
                        act.wait_ge(g_h, t * NE + (e + 1))
                        nc.scalar.activation(hr[:, 0, :], M1[:, 0:P], ACT.Relu).then_inc(g_relu, 1)
                        act.wait_ge(g_relu, t * NE + (e + 1))
                        nc.scalar.activation(hT[:, 0:P], hr[:, 0, :], ACT.Square).then_inc(g_hT, 1)

        @block.vector
        def _(dve):
            nc.vector.memset(qst[MROW:P, 0, :, :].bitcast(FP32), 0.0).then_inc(qst_zeroed, 1)

            def keys(part):
                for c in range(*KPARTS[part]):
                    for h in range(2):
                        n = 2 * c + h
                        dve.wait_ge(kth_ready, n + 1)
                        nc.vector.tensor_tensor(ktl[:, h, c * KC:(c + 1) * KC], key_bank[n % 4][:, 0:KC],
                                                kth[:, h, c * KC:(c + 1) * KC].bitcast(FP32), ALU.subtract).then_inc(ktl_ready, 1)

            links = []

            def link(ins):
                links.append(ins)
                ins.then_inc(top_step, 1)
                dve.wait_ge(top_step, len(links))

            first, second, gap, e_gap, many = (top[:, n, :] for n in range(5))
            wide = lambda t: t.unsqueeze(2).to_broadcast([P, t.shape[-1], NE])

            def gaps(b0, b1):
                n = slice(2 * b0, 2 * b1)
                dve.wait_ge(logits_ready, b1)
                link(nc.vector.tensor_reduce(first[:, n], logits[:, n, :], AX.X, ALU.max))
                link(nc.vector.tensor_tensor(prob[:, n, :], logits[:, n, :], wide(first[:, n]), ALU.is_ge))
                link(nc.vector.tensor_reduce(many[:, n], prob[:, n, :], AX.X, ALU.add))
                link(nc.vector.scalar_tensor_tensor(l2[:, n, :], prob[:, n, :], -BIG, logits[:, n, :], ALU.mult, ALU.add))
                link(nc.vector.tensor_reduce(second[:, n], l2[:, n, :], AX.X, ALU.max))
                link(nc.vector.tensor_tensor(gap[:, n], second[:, n], first[:, n], ALU.subtract))

            def weights():
                dve.wait_ge(gap_exp, 1)
                link(nc.vector.tensor_scalar(second, e_gap, 1.0, None, ALU.add))
                link(nc.vector.reciprocal(first, second))
                link(nc.vector.tensor_scalar(gap, first, 1.0, None, ALU.is_ge))
                link(nc.vector.scalar_tensor_tensor(first, many, 1.0, gap, ALU.is_equal, ALU.mult))
                link(nc.vector.tensor_tensor(prob[:, :, :], prob[:, :, :], wide(first), ALU.mult))
                link(nc.vector.tensor_reduce(any1[:, :], prob[:, :, :].rearrange("p n e -> p (n e)"), AX.X, ALU.max))

            def step(l, a, m, c, d, f, g):
                def low_part(j):
                    if not c.exists:
                        return
                    s0, n = GROUPS[j]
                    e = (6 * c.par + j) % 2
                    dve.wait_ge(ph_ready, c.at(6, j + 1))
                    if j >= 2 or (c - 1).exists:
                        dve.wait_ge(pv_done, c.at(6, j - 1))
                    nc.vector.tensor_tensor(pl[:, e, 0:n, :], E[:, e, 0:n, :], ph[:, e, 0:n, :], ALU.subtract).then_inc(pl_ready, 1)

                def maximum(b, j):
                    if not b.exists:
                        return
                    t, h = j // 2, j % 2
                    dve.wait_ge(sa_done, b.at(4, j + 1))
                    if j == 0 and (b - 1).exists:
                        dve.wait_ge(mT_done, (b - 1).at(1, 1))
                    src = psA[:, :].rearrange("p (g c) -> p g c", g=2)[:, :, 0:HG].rearrange("p g (h k) -> p g h k", k=NK)
                    nc.vector.tensor_reduce(nm[:, t, 8 * h:8 * h + 8].rearrange("p (g h) -> p g h", g=2), src, AX.X, ALU.max,
                                            negate=True).then_inc(max_ready, 1)

                def row_statistics(bt, st, own, used):
                    if (bt - 1).exists:
                        dve.wait_ge(used, (bt - 1).at(4, 4))
                    stand_alone(dve)
                    for j in range(2):
                        nc.vector.bn_stats(st[:, j, :], X[:, bass.ds(bt.index() * 2 + j, 1), :].rearrange("p a c -> p (a c)")).then_inc(own, 1)

                def mean_variance(bt, st, own, mv, stats):
                    dve.wait_ge(own, bt.at(2, 2))
                    stand_alone(dve)
                    for j in range(2):
                        nc.vector.bn_aggr(mv[:, j, :], st[:, j, :]).then_inc(stats, 1)

                if d.exists:
                    o = [psO[t][:, 0:H * OC].rearrange("p (h c) -> p h c", c=OC) for t in range(2)]
                    dve.wait_ge(pv_done, d.at(6, 6))
                    for t in range(2):
                        nc.vector.reciprocal(rden[:, t, :].unsqueeze(2), o[t][:, :, HD:OC]).then_inc(den_ready, 1)
                    for t in range(2):
                        dve.wait_ge(den_ready, d.at(2, t + 1))
                        if t == 0 and (d - 1).exists:
                            dve.wait_ge(oT_done, (d - 1).at(1, 1))
                        nc.vector.tensor_tensor(on[:, t, :].rearrange("p (h c) -> p h c", c=HD), o[t][:, :, 0:HD],
                                                rden[:, t, :].unsqueeze(2).to_broadcast([P, H, HD]), ALU.mult).then_inc(on_ready, 1)
                low_part(0)
                if g.exists:
                    dve.wait_ge(ffn_done, g.at(1, 1))
                    if (g - 2).exists:
                        dve.wait_ge(out_stored[g.par], (g - 2).at2(DMA))
                    nc.vector.tensor_tensor(ost[:, g.par, :, :], M1[:, :].rearrange("p (j c) -> p j c", j=2),
                                            X[:, bass.ds(g.index() * 2, 2), :], ALU.add).then_inc(out_ready, 1)
                    if isinstance(g.i, int) and g.k == NB - 2:
                        gaps(0, NB - 1)
                low_part(1)
                maximum(m, 2)
                if l.exists:
                    dve.wait_ge(x_in[l.par], l.at2(DMA))
                    row_statistics(l, st1, ln1_step, scale1)
                maximum(m, 3)
                low_part(2)
                if l.exists:
                    mean_variance(l, st1, ln1_step, mv1, stats1)
                if a.exists:
                    dve.wait_ge(qh_ready, a.at(1, 1))
                    if (a - 2).exists:
                        dve.wait_ge(qst_in[a.par], (a - 2).at2(2 * DMA))
                    nc.vector.tensor_tensor(ql[:, a.par, :, :], M1[:, :].rearrange("p (k q) -> p k q", k=2),
                                            qh[:, a.par, :, :].bitcast(FP32), ALU.subtract).then_inc(ql_ready, 1)
                if key_part(a) is not None:
                    keys(key_part(a))
                    if key_part(a) == 0:
                        nc.vector.memset(qst[MROW:P, 1, :, :].bitcast(FP32), 0.0).then_inc(qst_zeroed, 1)
                low_part(3)
                low_part(4)
                if m.exists:
                    dve.wait_ge(v_done, m.at(1, 1))
                    if (m - 1).exists:
                        dve.wait_ge(v_ready, (m - 1).at(4, 4))
                    nc.vector.tensor_tensor(vf[:, :, :], psA[:, 0:NBLK * HD].rearrange("p (n c) -> p n c", c=HD),
                                            mask[:, :].unsqueeze(2).to_broadcast([P, NBLK, HD]), ALU.mult).then_inc(v_masked, 1)
                if d.exists:
                    dve.wait_ge(attn_done, d.at(1, 1))
                    xt = X[:, bass.ds(d.index() * 2, 2), :]
                    nc.vector.tensor_tensor(xt, M0[:, :].rearrange("p (j c) -> p j c", j=2), xt, ALU.add).then_inc(y_ready, 1)
                maximum(a, 0)
                if d.exists:
                    dve.wait_ge(y_ready, d.at(1, 1))
                    row_statistics(d, st2, ln2_step, scale2)
                low_part(5)
                if f.exists:
                    dve.wait_ge(hr_ready, f.at(1, 1))
                    nc.vector.tensor_copy(logits[:, bass.ds(f.index() * 2, 2), :],
                                          M1[:, 0:2 * (F + NE)].rearrange("p (j f) -> p j f", j=2)[:, :, F:F + NE]).then_inc(logits_ready, 1)
                if d.exists:
                    mean_variance(d, st2, ln2_step, mv2, stats2)
                maximum(a, 1)

            schedule(dve, step, {NB + 2: lambda: gaps(NB - 1, NB)})
            weights()
            dve.wait_ge(any_done, 1)
            nc.vector.tensor_copy(flag[0:1, 0:1], M0[0:1, 0:1]).then_inc(flag_ready, 1)
            dve.wait_ge(flag_ready, 1)
            with dve.If(dve.value_load(flag[0:1, 0:1]) != 0):
                dve.sem_inc(g_added, 1)
                with dve.Fori(0, NT) as t:
                    dve.wait_ge(g_added, t * NE + 1)
                    stand_alone(dve)
                    nc.vector.bn_stats(st2[:, 0, :], X[:, bass.ds(t, 1), :].rearrange("p a c -> p (a c)")).then_inc(g_step, 1)
                    dve.wait_ge(g_step, t + 1)
                    stand_alone(dve)
                    nc.vector.bn_aggr(mv2[:, 0, :], st2[:, 0, :]).then_inc(g_stats, 1)
                    dve.wait_ge(g_out_in, t * DMA + DMA)
                    for e in range(NE):
                        dve.wait_ge(g_y, t * NE + (e + 1))
                        dve.wait_ge(g_added, t * NE + (e + 1))
                        nc.vector.scalar_tensor_tensor(gout[:, :], psS[0][:, 0:D],
                                                       prob[:, bass.ds(t, 1), e:e + 1].rearrange("p n e -> p (n e)"),
                                                       gout[:, :], ALU.mult, ALU.add).then_inc(g_added, 1)

        @block.tensor
        def _(pe):
            def keys(part):
                for c in range(*KPARTS[part]):
                    for h in range(2):
                        n = 2 * c + h
                        if n >= 4:
                            pe.wait_ge(ktl_ready, n - 3)
                        nc.tensor.matmul(key_bank[n % 4][:, 0:KC], wk[:, h * P:(h + 1) * P],
                                         z[:, KB * c:KB * (c + 1), :], start=True, stop=True).then_inc(kproj, 1)

            pe.wait_ge(consts_in, 2 * DMA)
            def step(l, a, m, c, d, f, g):
                def scores(j):
                    if not c.exists:
                        return
                    s0, n = GROUPS[j]
                    e = (6 * c.par + j) % 2
                    if j == 0:
                        pe.wait_ge(kst_in[c.par], c.at2(4 * DMA))
                        pe.wait_ge(qst_in[c.par], c.at2(2 * DMA))
                        pe.wait_ge(m_in[c.par], c.at2(DMA))
                    if j >= 2 or (c - 1).exists:
                        pe.wait_ge(ph_ready, c.at(6, j - 1))
                    for u in range(n):
                        last = nc.tensor.matmul(psS[e][:, u * S:(u + 1) * S], kst[:, c.par, s0 + u, :],
                                                qst[:, c.par, s0 + u, :], start=True, stop=True)
                    last.then_inc(s_done, 1)

                def values(j):
                    if not c.exists:
                        return
                    s0, n = GROUPS[j]
                    e = (6 * c.par + j) % 2
                    if j == 0:
                        pe.wait_ge(v_ready, c.at(4, 4))
                        if d.exists:
                            pe.wait_ge(on_ready, d.at(2, 2))
                    pe.wait_ge(pl_ready, c.at(6, j + 1))
                    for t in range(2):
                        for u in range(n):
                            s = s0 + u
                            nh, h0, blk = NHS[s], FIRST[s], VBLK[s]
                            o = psO[t][:, h0 * OC:(h0 + nh) * OC]
                            q = slice(t * P, (t + 1) * P)
                            for k, (p_, v_) in enumerate(((ph, v1), (ph, v2), (ph, v3), (pl, v1), (pl, v2))):
                                last = nc.tensor.matmul(o, p_[:, e, u, q],
                                                        v_[:, c.par, blk:blk + nh, :].rearrange("p n c -> p (n c)"),
                                                        start=(s == 0 and k == 0), stop=(s == NSL - 1 and k == 4),
                                                        skip_group_check=True)
                    last.then_inc(pv_done, 1)

                def maxima_scores(b, j):
                    if not b.exists:
                        return
                    t, h = j // 2, j % 2
                    if j == 0:
                        pe.wait_ge(kbd_ready, b.at(2, 2))
                        pe.wait_ge(qh_ready, b.at(1, 1))
                        if (b - 1).exists:
                            pe.wait_ge(v_masked, (b - 1).at(1, 1))
                    else:
                        pe.wait_ge(max_ready, b.at(4, j))
                    for u in range(2):
                        last = nc.tensor.matmul(psA[:, 512 * u:512 * u + HG], qh[:, b.par, h, t * P:(t + 1) * P],
                                                kbd[:, b.par, h, u * HG:(u + 1) * HG], start=True, stop=True)
                    last.then_inc(sa_done, 1)

                def transposes(dst, src, done):
                    for k in range(2):
                        for t in range(2):
                            last = nc.tensor.transpose(dst[:, k * S + t * P:k * S + (t + 1) * P],
                                                       src[:, t, k * P:(k + 1) * P], ident[:, :])
                    last.then_inc(done, 1)

                def project(dst, src, w, done):
                    n = w.shape[-1]
                    for t in range(2):
                        for k in range(2):
                            last = nc.tensor.matmul(dst[:, t * n:(t + 1) * n], src[:, k, t * P:(t + 1) * P], w[:, k, :],
                                                    start=(k == 0), stop=(k == 1))
                    last.then_inc(done, 1)

                scores(0)
                if g.exists:
                    pe.wait_ge(logits_ready, g.at(1, 1))
                    pe.wait_ge(hT_ready, g.at(1, 1))
                    for t in range(2):
                        last = nc.tensor.matmul(M1[:, t * D:(t + 1) * D], hT[:, t * P:(t + 1) * P], ws2[:, :],
                                                start=True, stop=True)
                    last.then_inc(ffn_done, 1)
                scores(1)
                maxima_scores(m, 2)
                if d.exists:
                    if g.exists:
                        pe.wait_ge(hT_ready, g.at(1, 1))
                    elif f.exists:
                        pe.wait_ge(y_ready, f.at(1, 1))
                    pe.wait_ge(on_ready, d.at(2, 2))
                    transposes(M0, on[:, :, :], oT_done)
                values(0)
                scores(2)
                if a.exists:
                    if g.exists:
                        pe.wait_ge(out_ready, g.at(1, 1))
                    elif (a - 1).exists:
                        pe.wait_ge(ql_ready, (a - 1).at(1, 1))
                    if isinstance(a.i, int) and a.k == 0:
                        pe.wait_ge(query_consts_in, 2 * DMA)
                    pe.wait_ge(xn_ready, a.at(1, 1))
                    transposes(M1, xn[:, :, :], xT_done)
                values(1)
                maxima_scores(m, 3)
                if a.exists:
                    pe.wait_ge(xnT_ready, a.at(1, 1))
                    for h in range(2):
                        for k in range(2):
                            last = nc.tensor.matmul(M1[:, h * S:(h + 1) * S], wq[:, k, h * P:(h + 1) * P], xnT[:, k, :],
                                                    start=(k == 0), stop=(k == 1))
                    last.then_inc(q_done, 1)
                if key_part(a) is not None:
                    if a.exists:
                        pe.wait_ge(z_rest_in, DMA)
                    keys(key_part(a))
                if isinstance(a.i, int) and a.k == 1:
                    pe.wait_ge(const1_in, NCONST * DMA)
                    pe.wait_ge(ktl_ready, 2 * NKC)
                scores(3)
                values(2)
                if m.exists:
                    pe.wait_ge(max_ready, m.at(4, 4))
                    for t in range(2):
                        last = nc.tensor.transpose(psA[0:H, t * P:(t + 1) * P], nm[:, t, :], ident[:, :])
                    last.then_inc(mT_done, 1)
                scores(4)
                if d.exists:
                    pe.wait_ge(onT_ready, d.at(1, 1))
                    project(M0, onT, wo, attn_done)
                if m.exists:
                    n_a = 11 * HD
                    pe.wait_ge(mh_ready, m.at(1, 1))
                    pe.wait_ge(zc_in[m.par], m.at2(DMA))
                    nc.tensor.matmul(psA[:, 0:n_a], zc[:, m.par, 0:P], wv[:, 0:n_a], start=True, stop=True)
                    nc.tensor.matmul(psA[:, n_a:NBLK * HD], zc[:, m.par, CUT:CUT + P], wv[:, n_a:NBLK * HD],
                                     start=True, stop=True).then_inc(v_done, 1)
                if f.exists:
                    if a.exists:
                        pe.wait_ge(ql_ready, a.at(1, 1))
                    elif g.exists:
                        pe.wait_ge(out_ready, g.at(1, 1))
                    pe.wait_ge(yn_ready, f.at(1, 1))
                    transposes(M1, yn[:, :, :], yT_done)
                scores(5)
                values(3)
                maxima_scores(a, 0)
                if f.exists:
                    pe.wait_ge(ynT_ready, f.at(1, 1))
                    project(M1, ynT, w1r, h_done)
                values(4)
                if f.exists:
                    if d.exists:
                        pe.wait_ge(y_ready, d.at(1, 1))
                    else:
                        pe.wait_ge(hT_ready, g.at(1, 1))
                    pe.wait_ge(hr_ready, f.at(1, 1))
                    for t in range(2):
                        last = nc.tensor.transpose(M0[:, t * P:(t + 1) * P], hr[:, t, :], ident[:, :])
                    last.then_inc(hT_done, 1)
                maxima_scores(a, 1)
                values(5)

            schedule(pe, step)
            pe.wait_ge(top_step, 18)
            pe.wait_ge(hT_ready, NB)
            nc.tensor.matmul(M0[0:1, 0:1], any1[:, :], ones[:, :], start=True, stop=True).then_inc(any_done, 1)
            pe.wait_ge(flag_ready, 1)
            with pe.If(pe.value_load(flag[0:1, 0:1]) != 0):
                pe.wait_ge(experts_in, 2 * DMA)
                with pe.Fori(0, NT) as t:
                    pe.wait_ge(g_yn, t + 1)
                    for k in range(2):
                        last = nc.tensor.transpose(M0[:, k * P:(k + 1) * P], yn[:, 0, k * P:(k + 1) * P], ident[:, :])
                    last.then_inc(g_yT, 1)
                    pe.wait_ge(g_ynT, t + 1)
                    for e in range(NE):
                        pe.wait_ge(g_hT, t * NE + (e + 1))
                        for k in range(2):
                            last = nc.tensor.matmul(M1[:, 0:P], w1[:, k, e, :], ynT[:, k, 0:P], start=(k == 0), stop=(k == 1))
                        last.then_inc(g_h, 1)
                        pe.wait_ge(g_hT, t * NE + (e + 2))
                        pe.wait_ge(g_added, t * NE + (e + 1))
                        nc.tensor.matmul(psS[0][:, 0:D], hT[:, 0:P], w2[:, e, :], start=True, stop=True).then_inc(g_y, 1)


def kernel(x, ctx_512, L0_xattn_Wq, L0_xattn_Wkv, L0_xattn_Wo, L0_ffn_Ws1, L0_ffn_Ws2, L0_ffn_W1, L0_ffn_W2,
           L0_ffn_Wr):
    import numpy as np
    import concourse.bacc as bacc
    from concourse.bass_utils import run_bass_kernel_spmd

    f32 = np.float32
    cols = lambda w: w.reshape(2, P, -1).transpose(1, 0, 2)
    zt = ctx_512.transpose(2, 0, 1)
    wvt = L0_xattn_Wkv[D:].T.reshape(LAT, H, HD)
    order = [h for i in range(6) for h in (3 * i, 3 * i + 1) if h < H] + [h for i in range(5) for h in (3 * i + 1, 3 * i + 2)]
    row = np.arange(P)
    mask = np.zeros((P, NBLK), f32)
    sel = np.zeros((2, H, NSL, P), f32)
    for s in range(NSL):
        spans = ((0, NK), (NK, P)) if s % 2 == 0 else ((0, REST), (REST, REST + NK))
        for n in range(NHS[s]):
            own = (row >= spans[n][0]) & (row < spans[n][1])
            mask[:, VBLK[s] + n] = own
            sel[0, FIRST[s] + n, s, :] = own
    arrays = {
        "x": x.reshape(NB * S, D),
        "z": zt,
        "zz": np.concatenate([zt, zt, zt[:, :, :REST]], axis=2),
        "wq": cols(L0_xattn_Wq.T),
        "wk": L0_xattn_Wkv[:D].T,
        "wv": wvt[:, order, :].reshape(LAT, NBLK * HD),
        "wo": cols(L0_xattn_Wo.T),
        "w1r": cols(np.concatenate([L0_ffn_Ws1, L0_ffn_Wr], axis=1)),
        "ws2": L0_ffn_Ws2,
        "w1": L0_ffn_W1.reshape(NE, 2, P, F).transpose(2, 1, 0, 3),
        "w2": L0_ffn_W2.transpose(1, 0, 2),
        "ident": np.eye(P, dtype=f32),
        "mask": mask,
        "headmask": (row[:, None] // HD == np.arange(8)).astype(f32),
        "sel": sel.reshape(32, NSL * P),
    }
    arrays = {n: np.ascontiguousarray(a) for n, a in arrays.items()}
    nc = bacc.Bacc("TRN2", target_bir_lowering=False, num_devices=1)
    args = [nc.dram_tensor(f"in_{n}", a.shape, FP32, kind="ExternalInput").ap() for n, a in arrays.items()]
    out = nc.dram_tensor("out", (NB * S, D), FP32, kind="ExternalOutput").ap()
    build(nc, *args, out)
    r = run_bass_kernel_spmd(nc, [{f"in_{n}": a for n, a in arrays.items()}], core_ids=[0])
    return r.results[0]["out"].reshape(NB, S, D)
```
